# Optimizing a Trainium2 kernel written in Bass

```python
import numpy as np
import jax
import jax.numpy as jnp

def _softmax(x, axis=-1):
    return jax.nn.softmax(x, axis=axis)

def _gelu(x):
    return jax.nn.gelu(x, approximate=True)

def _silu(x):
    return jax.nn.silu(x)

def _sigmoid(x):
    return jax.nn.sigmoid(x)

def _layernorm(x, axis=-1, eps=1e-05):
    m = jnp.mean(x, axis=axis, keepdims=True)
    v = jnp.var(x, axis=axis, keepdims=True)
    return (x - m) / jnp.sqrt(v + eps)

def _scatter_add(tgt, idx, src, axis=0):
    return tgt.at[idx].add(src)

def _segment_sum(src, seg, n):
    return jax.ops.segment_sum(src, seg, n)
kernel_name = 'mk_seq_postln_d1_jaxref_r8_7d66d2'

def setup_inputs(seed: int=0):
    np.random.seed(seed)
    _w = jnp.asarray

    def _L0_attn_setup():
        import jax, jax.numpy as jnp
        import numpy as np
        from jax import lax
        D_MODEL = 256
        D_STATE = 64
        D_CONV = 4
        EXPAND = 2
        HEADDIM = 64
        D_INNER = D_MODEL * EXPAND
        NHEADS = D_INNER // HEADDIM
        CONV_DIM = D_INNER + 2 * D_STATE
        D_IN_PROJ = 2 * D_INNER + 2 * D_STATE + NHEADS
        NUM_EXPERTS = 8
        TOP_K = 2
        D_FF = 4 * D_MODEL
        BATCH = 2
        SEQ = 64
        EPS = 1e-06

        def rmsnorm(x, w):
            return x * lax.rsqrt(jnp.mean(x * x, axis=-1, keepdims=True) + EPS) * w

        def silu(x):
            return x * jax.nn.sigmoid(x)

        def mamba2(x, in_proj_w, conv_w, conv_b, dt_bias, A_log, Dp, ssm_norm_w, out_proj_w):
            Bsz, L, _ = x.shape
            zxbcdt = x @ in_proj_w.T
            z, xBC, dt = jnp.split(zxbcdt, [D_INNER, D_INNER + CONV_DIM], axis=-1)
            xBC = lax.conv_general_dilated(xBC.transpose(0, 2, 1), conv_w[:, None, :], (1,), [(D_CONV - 1, 0)], feature_group_count=CONV_DIM)
            xBC = silu((xBC + conv_b[None, :, None]).transpose(0, 2, 1))
            xs, Bm, Cm = jnp.split(xBC, [D_INNER, D_INNER + D_STATE], axis=-1)
            dt = jax.nn.softplus(dt + dt_bias)
            A = -jnp.exp(A_log)
            xh = xs.reshape(Bsz, L, NHEADS, HEADDIM)

            def step(h, inp):
                dt_t, x_t, B_t, C_t = inp
                dA = jnp.exp(dt_t * A)
                h = h * dA[:, :, None, None] + dt_t[:, :, None, None] * x_t[..., None] * B_t[:, None, None, :]
                y = jnp.einsum('bhpn,bn->bhp', h, C_t)
                return (h, y)
            h0 = jnp.zeros((Bsz, NHEADS, HEADDIM, D_STATE), x.dtype)
            _, ys = lax.scan(step, h0, (dt.transpose(1, 0, 2), xh.transpose(1, 0, 2, 3), Bm.transpose(1, 0, 2), Cm.transpose(1, 0, 2)))
            y = ys.transpose(1, 0, 2, 3) + Dp[None, None, :, None] * xh
            y = y.reshape(Bsz, L, D_INNER)
            y = rmsnorm(y * silu(z), ssm_norm_w)
            return y @ out_proj_w.T

        def moe(x, gate_w, w1, w2):
            T = x.shape[0] * x.shape[1]
            xf = x.reshape(T, D_MODEL)
            logits = xf @ gate_w.T
            vals, idx = lax.top_k(logits, TOP_K)
            wts = jax.nn.softmax(vals, axis=-1)
            combine = jnp.sum(jax.nn.one_hot(idx, NUM_EXPERTS, dtype=x.dtype) * wts[..., None], axis=1)
            h = silu(jnp.einsum('td,efd->tef', xf, w1))
            eo = jnp.einsum('tef,edf->ted', h, w2)
            out = jnp.einsum('ted,te->td', eo, combine)
            probs = jax.nn.softmax(logits, axis=-1)
            lb = NUM_EXPERTS * jnp.sum(jnp.mean(probs, axis=0) ** 2)
            return (out.reshape(x.shape), lb)

        def safety(x, sp1_w, sp1_b, sp2_w, sp2_b, harm_w, harm_b, unc_w, unc_b, tox_w, tox_b):
            f = silu(x @ sp1_w.T + sp1_b) @ sp2_w.T + sp2_b
            harm = f @ harm_w.T + harm_b
            unc = jax.nn.sigmoid(f @ unc_w.T + unc_b)[..., 0]
            tox = jax.nn.sigmoid(f @ tox_w.T + tox_b)[..., 0]
            hs = jax.nn.sigmoid(harm)
            return (hs.max(-1), jnp.argmax(hs, -1), unc, tox, harm)

        def _reference_tuple_inner(x, in_proj_w, conv_w, conv_b, dt_bias, A_log, D, ssm_norm_w, out_proj_w, norm_mamba_w, norm_moe_w, gate_w, w1, w2, sp1_w, sp1_b, sp2_w, sp2_b, harm_w, harm_b, unc_w, unc_b, tox_w, tox_b):
            residual = x
            h = rmsnorm(x, norm_mamba_w)
            h = mamba2(h, in_proj_w, conv_w, conv_b, dt_bias, A_log, D, ssm_norm_w, out_proj_w) + residual
            x_moe, lb_loss = moe(rmsnorm(h, norm_moe_w), gate_w, w1, w2)
            h = h + x_moe
            risk_vals, risk_idx, unc, tox, harm = safety(h, sp1_w, sp1_b, sp2_w, sp2_b, harm_w, harm_b, unc_w, unc_b, tox_w, tox_b)
            return (h, risk_vals, risk_idx, unc, tox, harm, lb_loss)
        ks = jax.random.split(jax.random.key(seed), 24)
        s = 0.02
        n = lambda k, shape, sc=s: jax.random.normal(k, shape, jnp.float32) * sc
        return {'x': jax.random.normal(ks[0], (BATCH, SEQ, D_MODEL), jnp.float32), 'in_proj_w': n(ks[1], (D_IN_PROJ, D_MODEL)), 'conv_w': n(ks[2], (CONV_DIM, D_CONV), 0.1), 'conv_b': n(ks[3], (CONV_DIM,), 0.01), 'dt_bias': n(ks[4], (NHEADS,), 0.1), 'A_log': jnp.log(jax.random.uniform(ks[5], (NHEADS,), jnp.float32, 1.0, 16.0)), 'D': jnp.ones((NHEADS,), jnp.float32), 'ssm_norm_w': jnp.ones((D_INNER,), jnp.float32), 'out_proj_w': n(ks[6], (D_MODEL, D_INNER)), 'norm_mamba_w': jnp.ones((D_MODEL,), jnp.float32), 'norm_moe_w': jnp.ones((D_MODEL,), jnp.float32), 'gate_w': n(ks[7], (NUM_EXPERTS, D_MODEL)), 'w1': n(ks[8], (NUM_EXPERTS, D_FF, D_MODEL)), 'w2': n(ks[9], (NUM_EXPERTS, D_MODEL, D_FF)), 'sp1_w': n(ks[10], (D_MODEL // 2, D_MODEL)), 'sp1_b': jnp.zeros((D_MODEL // 2,), jnp.float32), 'sp2_w': n(ks[11], (128, D_MODEL // 2)), 'sp2_b': jnp.zeros((128,), jnp.float32), 'harm_w': n(ks[12], (5, 128)), 'harm_b': jnp.zeros((5,), jnp.float32), 'unc_w': n(ks[13], (1, 128)), 'unc_b': jnp.zeros((1,), jnp.float32), 'tox_w': n(ks[14], (1, 128)), 'tox_b': jnp.zeros((1,), jnp.float32)}
    _L0_attn_in = _L0_attn_setup()

    def _L0_ffn_setup():
        import jax, jax.numpy as jnp
        import numpy as np
        HIDDEN = 256
        INTER = 1024
        B, S = (4, 128)

        def _qmatmul(x, w_int8, scale):
            y = jnp.einsum('bsh,ho->bso', x, w_int8.astype(x.dtype))
            return y * scale
        key = jax.random.key(seed)
        ks = jax.random.split(key, 7)
        x = jax.random.normal(ks[0], (B, S, HIDDEN), dtype=jnp.float32)
        w_gate = jax.random.randint(ks[1], (HIDDEN, INTER), -128, 128, dtype=jnp.int32).astype(jnp.int8)
        w_up = jax.random.randint(ks[2], (HIDDEN, INTER), -128, 128, dtype=jnp.int32).astype(jnp.int8)
        w_down = jax.random.randint(ks[3], (INTER, HIDDEN), -128, 128, dtype=jnp.int32).astype(jnp.int8)
        s_gate = jax.random.uniform(ks[4], (INTER,), dtype=jnp.float32) * 0.02 + 0.001
        s_up = jax.random.uniform(ks[5], (INTER,), dtype=jnp.float32) * 0.02 + 0.001
        s_down = jax.random.uniform(ks[6], (HIDDEN,), dtype=jnp.float32) * 0.02 + 0.001
        return {'x': x, 'w_gate': w_gate, 'w_up': w_up, 'w_down': w_down, 's_gate': s_gate, 's_up': s_up, 's_down': s_down}
    _L0_ffn_in = _L0_ffn_setup()
    _d = {'L0_attn_x': _L0_attn_in['x'], 'L0_attn_in_proj_w': _L0_attn_in['in_proj_w'], 'L0_attn_conv_w': _L0_attn_in['conv_w'], 'L0_attn_conv_b': _L0_attn_in['conv_b'], 'L0_attn_dt_bias': _L0_attn_in['dt_bias'], 'L0_attn_A_log': _L0_attn_in['A_log'], 'L0_attn_D': _L0_attn_in['D'], 'L0_attn_ssm_norm_w': _L0_attn_in['ssm_norm_w'], 'L0_attn_out_proj_w': _L0_attn_in['out_proj_w'], 'L0_attn_norm_mamba_w': _L0_attn_in['norm_mamba_w'], 'L0_attn_norm_moe_w': _L0_attn_in['norm_moe_w'], 'L0_attn_gate_w': _L0_attn_in['gate_w'], 'L0_attn_w1': _L0_attn_in['w1'], 'L0_attn_w2': _L0_attn_in['w2'], 'L0_attn_sp1_w': _L0_attn_in['sp1_w'], 'L0_attn_sp1_b': _L0_attn_in['sp1_b'], 'L0_attn_sp2_w': _L0_attn_in['sp2_w'], 'L0_attn_sp2_b': _L0_attn_in['sp2_b'], 'L0_attn_harm_w': _L0_attn_in['harm_w'], 'L0_attn_harm_b': _L0_attn_in['harm_b'], 'L0_attn_unc_w': _L0_attn_in['unc_w'], 'L0_attn_unc_b': _L0_attn_in['unc_b'], 'L0_attn_tox_w': _L0_attn_in['tox_w'], 'L0_attn_tox_b': _L0_attn_in['tox_b'], 'L0_ffn_w_gate': _L0_ffn_in['w_gate'], 'L0_ffn_w_up': _L0_ffn_in['w_up'], 'L0_ffn_w_down': _L0_ffn_in['w_down'], 'L0_ffn_s_gate': _L0_ffn_in['s_gate'], 'L0_ffn_s_up': _L0_ffn_in['s_up'], 'L0_ffn_s_down': _L0_ffn_in['s_down']}
    _x0 = _d['L0_attn_x']
    _d['L0_attn_x'] = jax.random.normal(jax.random.fold_in(jax.random.key(seed), 1), (4, 1024, 256), dtype=_x0.dtype)
    del _x0
    return _d

def reference(L0_attn_x, L0_attn_in_proj_w, L0_attn_conv_w, L0_attn_conv_b, L0_attn_dt_bias, L0_attn_A_log, L0_attn_D, L0_attn_ssm_norm_w, L0_attn_out_proj_w, L0_attn_norm_mamba_w, L0_attn_norm_moe_w, L0_attn_gate_w, L0_attn_w1, L0_attn_w2, L0_attn_sp1_w, L0_attn_sp1_b, L0_attn_sp2_w, L0_attn_sp2_b, L0_attn_harm_w, L0_attn_harm_b, L0_attn_unc_w, L0_attn_unc_b, L0_attn_tox_w, L0_attn_tox_b, L0_ffn_w_gate, L0_ffn_w_up, L0_ffn_w_down, L0_ffn_s_gate, L0_ffn_s_up, L0_ffn_s_down):

    def _L0_attn_ref(x, in_proj_w, conv_w, conv_b, dt_bias, A_log, D, ssm_norm_w, out_proj_w, norm_mamba_w, norm_moe_w, gate_w, w1, w2, sp1_w, sp1_b, sp2_w, sp2_b, harm_w, harm_b, unc_w, unc_b, tox_w, tox_b):
        import jax, jax.numpy as jnp
        import numpy as np
        from jax import lax
        D_MODEL = 256
        D_STATE = 64
        D_CONV = 4
        EXPAND = 2
        HEADDIM = 64
        D_INNER = D_MODEL * EXPAND
        NHEADS = D_INNER // HEADDIM
        CONV_DIM = D_INNER + 2 * D_STATE
        D_IN_PROJ = 2 * D_INNER + 2 * D_STATE + NHEADS
        NUM_EXPERTS = 8
        TOP_K = 2
        D_FF = 4 * D_MODEL
        BATCH = 2
        SEQ = 64
        EPS = 1e-06

        def rmsnorm(x, w):
            return x * lax.rsqrt(jnp.mean(x * x, axis=-1, keepdims=True) + EPS) * w

        def silu(x):
            return x * jax.nn.sigmoid(x)

        def mamba2(x, in_proj_w, conv_w, conv_b, dt_bias, A_log, Dp, ssm_norm_w, out_proj_w):
            Bsz, L, _ = x.shape
            zxbcdt = x @ in_proj_w.T
            z, xBC, dt = jnp.split(zxbcdt, [D_INNER, D_INNER + CONV_DIM], axis=-1)
            xBC = lax.conv_general_dilated(xBC.transpose(0, 2, 1), conv_w[:, None, :], (1,), [(D_CONV - 1, 0)], feature_group_count=CONV_DIM)
            xBC = silu((xBC + conv_b[None, :, None]).transpose(0, 2, 1))
            xs, Bm, Cm = jnp.split(xBC, [D_INNER, D_INNER + D_STATE], axis=-1)
            dt = jax.nn.softplus(dt + dt_bias)
            A = -jnp.exp(A_log)
            xh = xs.reshape(Bsz, L, NHEADS, HEADDIM)

            def step(h, inp):
                dt_t, x_t, B_t, C_t = inp
                dA = jnp.exp(dt_t * A)
                h = h * dA[:, :, None, None] + dt_t[:, :, None, None] * x_t[..., None] * B_t[:, None, None, :]
                y = jnp.einsum('bhpn,bn->bhp', h, C_t)
                return (h, y)
            h0 = jnp.zeros((Bsz, NHEADS, HEADDIM, D_STATE), x.dtype)
            _, ys = lax.scan(step, h0, (dt.transpose(1, 0, 2), xh.transpose(1, 0, 2, 3), Bm.transpose(1, 0, 2), Cm.transpose(1, 0, 2)))
            y = ys.transpose(1, 0, 2, 3) + Dp[None, None, :, None] * xh
            y = y.reshape(Bsz, L, D_INNER)
            y = rmsnorm(y * silu(z), ssm_norm_w)
            return y @ out_proj_w.T

        def moe(x, gate_w, w1, w2):
            T = x.shape[0] * x.shape[1]
            xf = x.reshape(T, D_MODEL)
            logits = xf @ gate_w.T
            vals, idx = lax.top_k(logits, TOP_K)
            wts = jax.nn.softmax(vals, axis=-1)
            combine = jnp.sum(jax.nn.one_hot(idx, NUM_EXPERTS, dtype=x.dtype) * wts[..., None], axis=1)
            h = silu(jnp.einsum('td,efd->tef', xf, w1))
            eo = jnp.einsum('tef,edf->ted', h, w2)
            out = jnp.einsum('ted,te->td', eo, combine)
            probs = jax.nn.softmax(logits, axis=-1)
            lb = NUM_EXPERTS * jnp.sum(jnp.mean(probs, axis=0) ** 2)
            return (out.reshape(x.shape), lb)

        def safety(x, sp1_w, sp1_b, sp2_w, sp2_b, harm_w, harm_b, unc_w, unc_b, tox_w, tox_b):
            f = silu(x @ sp1_w.T + sp1_b) @ sp2_w.T + sp2_b
            harm = f @ harm_w.T + harm_b
            unc = jax.nn.sigmoid(f @ unc_w.T + unc_b)[..., 0]
            tox = jax.nn.sigmoid(f @ tox_w.T + tox_b)[..., 0]
            hs = jax.nn.sigmoid(harm)
            return (hs.max(-1), jnp.argmax(hs, -1), unc, tox, harm)

        def _reference_tuple_inner(x, in_proj_w, conv_w, conv_b, dt_bias, A_log, D, ssm_norm_w, out_proj_w, norm_mamba_w, norm_moe_w, gate_w, w1, w2, sp1_w, sp1_b, sp2_w, sp2_b, harm_w, harm_b, unc_w, unc_b, tox_w, tox_b):
            residual = x
            h = rmsnorm(x, norm_mamba_w)
            h = mamba2(h, in_proj_w, conv_w, conv_b, dt_bias, A_log, D, ssm_norm_w, out_proj_w) + residual
            x_moe, lb_loss = moe(rmsnorm(h, norm_moe_w), gate_w, w1, w2)
            h = h + x_moe
            risk_vals, risk_idx, unc, tox, harm = safety(h, sp1_w, sp1_b, sp2_w, sp2_b, harm_w, harm_b, unc_w, unc_b, tox_w, tox_b)
            return (h, risk_vals, risk_idx, unc, tox, harm, lb_loss)
        return _reference_tuple_inner(x, in_proj_w, conv_w, conv_b, dt_bias, A_log, D, ssm_norm_w, out_proj_w, norm_mamba_w, norm_moe_w, gate_w, w1, w2, sp1_w, sp1_b, sp2_w, sp2_b, harm_w, harm_b, unc_w, unc_b, tox_w, tox_b)[0]

    def _L0_ffn_ref(x, w_gate, w_up, w_down, s_gate, s_up, s_down):
        import jax, jax.numpy as jnp
        import numpy as np
        HIDDEN = 256
        INTER = 1024
        B, S = (4, 128)

        def _qmatmul(x, w_int8, scale):
            y = jnp.einsum('bsh,ho->bso', x, w_int8.astype(x.dtype))
            return y * scale
        gate = jax.nn.silu(_qmatmul(x, w_gate, s_gate))
        up = _qmatmul(x, w_up, s_up)
        fuse = gate * up
        return _qmatmul(fuse, w_down, s_down)
    x = L0_attn_x
    x = _layernorm(x + _L0_attn_ref(x, L0_attn_in_proj_w, L0_attn_conv_w, L0_attn_conv_b, L0_attn_dt_bias, L0_attn_A_log, L0_attn_D, L0_attn_ssm_norm_w, L0_attn_out_proj_w, L0_attn_norm_mamba_w, L0_attn_norm_moe_w, L0_attn_gate_w, L0_attn_w1, L0_attn_w2, L0_attn_sp1_w, L0_attn_sp1_b, L0_attn_sp2_w, L0_attn_sp2_b, L0_attn_harm_w, L0_attn_harm_b, L0_attn_unc_w, L0_attn_unc_b, L0_attn_tox_w, L0_attn_tox_b), axis=-1)
    x = _layernorm(x + _L0_ffn_ref(x, L0_ffn_w_gate, L0_ffn_w_up, L0_ffn_w_down, L0_ffn_s_gate, L0_ffn_s_up, L0_ffn_s_down), axis=-1)
    return x

_drawn_inputs = setup_inputs


def setup_inputs(seed=0):
    import zlib

    import numpy as np

    out = dict(_drawn_inputs(seed))
    spreads = {'L0_attn_D': (1.0, 0.2),
     'L0_attn_ssm_norm_w': (1.0, 0.2),
     'L0_attn_norm_mamba_w': (1.0, 0.2),
     'L0_attn_norm_moe_w': (1.0, 0.6),
     'L0_attn_sp1_b': (0.0, 0.1),
     'L0_attn_sp2_b': (0.0, 0.1),
     'L0_attn_harm_b': (0.0, 0.1)}
    factors = {'L0_attn_dt_bias': 200.0, 'L0_attn_A_log': 64.0}
    for name, (base, spread) in spreads.items():
        noise = np.random.default_rng([zlib.crc32(name.encode()), seed]).standard_normal(out[name].shape)
        drawn = base * np.exp(spread * noise) if base else spread * noise
        out[name] = jnp.asarray(drawn.astype(out[name].dtype))
    for name, factor in factors.items():
        out[name] = (out[name] * factor).astype(out[name].dtype)
    return out
```

```python
from contextlib import ExitStack

import concourse.bass as bass
from concourse import mybir

F32 = mybir.dt.float32
F32R = mybir.dt.float32r
I32 = mybir.dt.int32
U32 = mybir.dt.uint32
I8 = mybir.dt.int8
ALU = mybir.AluOpType
ACT = mybir.ActivationFunctionType
AX = mybir.AxisListType

P = 128
D = 256
KD = D // P
B, L = 4, 1024
T = B * L
DI = 512
KI = DI // P
NS = 64
NH = 8
HD = DI // NH
CONV = DI + 2 * NS
KC = CONV // P
TAPS = 4
PROJ = 2 * DI + 2 * NS + NH
COL_X, COL_BC, COL_DT = DI, 2 * DI, 2 * DI + 2 * NS
GT = 512
CH = GT // P
NG = T // GT
NE = 8
FF = 1024
KF = FF // P
ROWS = 256
RT = ROWS // P
REGION = T + ROWS
RMS_EPS = 1e-6
LN_EPS = 1e-5
A_LOG_MAX = 80.0
DECAY_MIN = -1e30
SMALL = 1.0 / 64

SOFT_LINKS = 11
ROUTE_LINKS = 14
SMALL_DMAS = 8 + 2 * CH
TILES = KC + KI
ITEMS, FIRST, PAD_ROW, TABLE = 0, NE + 1, 2 * NE + 2, 3 * NE + 2


def bcast(ap, dim, n):
    ap = ap.unsqueeze(dim)
    shape = list(ap.shape)
    shape[dim] = n
    return ap.to_broadcast(shape)


def flat(ap):
    return ap.rearrange("p a b -> p (a b)")


def wait(eng, sem, value):
    if not (isinstance(value, int) and value == 0):
        eng.wait_ge(sem, value)


FFN_W = 2 * KD * FF + KF * D
MAX_ITEMS = 2 * T // ROWS + NE
MIX_LINKS, Y_LINKS = 4, 3


class Pass:

    def __init__(self, eng, sem):
        self.eng, self.sem, self.times, self.total = eng, sem, 1, 0

    def __call__(self):
        self.eng.sem_inc(self.sem, 1)
        self.total += self.times

    def done(self):
        self.eng.wait_ge(self.sem, self.total)


class Link:

    def __init__(self, eng, sem, base):
        self.eng, self.sem, self.base, self.n = eng, sem, base, 0

    def __call__(self, instruction, passed=None):
        self.n += 1
        instruction.then_inc(self.sem, 1)
        self.eng.wait_ge(self.sem, self.base + self.n)
        if passed:
            passed()


def mamba_phase(nc, io, dram, cst, routing):
    with ExitStack() as ctx:
        def sb(name, shape, dt=F32):
            return ctx.enter_context(nc.sbuf_tensor(name, shape, dt))

        def sem(name):
            return ctx.enter_context(nc.semaphore(name))

        ident, le, gt, lt, ones = cst["ident"], cst["le"], cst["gt"], cst["lt"], cst["ones"]
        half, zero1 = cst["half"], cst["zero1"]
        w_hi = sb("w_hi", [P, KD, PROJ], F32R)
        w_lo = sb("w_lo", [P, KD, PROJ], F32R)
        w_out = sb("w_out", [P, KI, D])
        gate_w = sb("gate_w", [P, KD, NE])
        ssm_w = sb("ssm_w", [P, KI])
        nm_w = sb("nm_w", [P, KD])
        moe_w = cst["moe_w"]
        conv_w = sb("conv_w", [P, KC, TAPS])
        conv_b = sb("conv_b", [P, KC])
        d_col = sb("d_col", [P, KI])
        dt_bias = sb("dt_bias", [P, CH, NH])
        a_log = sb("a_log", [P, CH, NH])
        a_neg = sb("a_neg", [P, CH, NH])
        x_in = sb("x_in", [P, 2, CH, D])
        squares = sb("squares", [P, CH, D])
        tail_squares = sb("tail_squares", [P, D])
        stat = sb("stat", [P, 3, CH])
        x_norm = sb("x_norm", [P, CH, D])
        h_hi = sb("h_hi", [P, KD, GT], F32R)
        h_lo = sb("h_lo", [P, KD, GT], F32R)
        soft = sb("soft", [P, 8, CH * NH])
        dt = sb("dt", [P, 2, CH * NH])
        la = sb("la", [P, CH * NH])
        pex = sb("pex", [P, 2, 3, CH * NH])
        la_t = sb("la_t", [P, NH, P])
        decay = sb("decay", [P, 2, CH, NH, P])
        raw = sb("raw", [P, 2, KC, TAPS - 1 + GT])
        conv = sb("conv", [P, 2, GT])
        xbc = sb("xbc", [P, 2, KC, GT])
        c_low = sb("c_low", [NS, 2, GT])
        z_act = sb("z_act", [P, 2, KI, GT])
        cb = sb("cb", [P, P])
        b_tok = sb("b_tok", [P, NS])
        x_dt = sb("x_dt", [P, NH, HD])
        x_end = sb("x_end", [P, NH, HD])
        state = sb("state", [NS, NH, HD])
        state_p = sb("state_p", [NS, NH, HD])
        y_in = sb("y_in", [P, NH, HD])
        y_tok = sb("y_tok", [P, NH, HD])
        y_d = sb("y_d", [P, KI, P])
        y_gated = sb("y_gated", [P, KI, P])
        y_sq = sb("y_sq", [P, KI, P])
        tail_stat = sb("tail_stat", [P, 8])
        h1 = sb("h1", [P, D])
        x_res = sb("x_res", [P, 2, CH, D])
        xm = sb("xm", [P, 2, CH, D])
        xm_t = sb("xm_t", [P, KD, P])
        logits = sb("logits", [P, CH, NE])
        top = sb("top", [P, CH, 8])
        top_i = sb("top_i", [P, CH, 8], U32)
        top_f = sb("top_f", [P, CH, 8])
        hot = sb("hot", [P, 3, CH, NE])
        run = sb("run", [P, CH + 1, NE])
        rank = sb("rank", [P, CH, NE])
        picked = sb("picked", [P, 2, CH, NE])
        row_f = sb("row_f", [P, CH, 2])
        row_u = sb("row_u", [P, 2, CH * 2], U32)
        iota_e = sb("iota_e", [P, NE])
        base_e = sb("base_e", [P, NE])
        items_i = sb("items_i", [P, NE], I32)
        rows_all, gap_all = routing["rows"], routing["gap"]

        bank = [ctx.enter_context(nc.psum_tensor(f"bank{i}", [P, 512], F32)) for i in range(8)]
        proj_ps = bank[0:2]
        dt_ps, cum_ps, rank_ps = bank[0][:, 0:32], bank[0][:, 0:96], bank[1][:, 0:64]
        out_ps, ss_ps = bank[2][:, 0:D], bank[2][:, D:D + 1]
        xmt_ps, logit_ps = bank[2][:, D:2 * D], bank[2][:, 0:NE]
        x_ps = bank[3]
        yt_ps, intra_ps, inter_ps = bank[4], bank[5], bank[6]
        cb_ps, bt_ps = bank[7][:, 0:P], bank[7][:, P:2 * P]

        s = {n: sem(n) for n in (
            "weights_in", "small_in", "masks", "w_split", "w_scaled", "a_exp", "a_ready", "iota_ready",
            "x_loaded", "ss_ready", "ms_ready", "rs_ready", "xn_ready", "ht_ps", "h_hi_ready",
            "h_lo_ready", "dt_done", "soft_in", "soft_exp", "soft_link", "la_ready", "cum_done",
            "pex_ready", "lat_ready", "seg_ps", "decay_ready", "tile_ps", "tile_out", "conv_link",
            "conv_ready", "xbc_ready", "c_moved", "halo_ready", "state_zero",
            "s1_done", "b_ready", "cb_ready", "xdt_ready", "m_ready", "xend_ready", "statep_ready",
            "inter_done", "intra_done", "state_done", "state_ready", "yin_ready", "ytok_ready",
            "yt_done", "yd_ready", "yg_ready", "ysq_ready", "out_done", "ms2_ready", "rs2_ready",
            "h1_ready", "xres_ready", "ss3_ready", "ms3_ready", "rs3_ready", "xm_ready", "xmt_done",
            "xmt_ready", "logit_done", "logit_ready", "route_link", "hot_ready", "rank_done",
            "rows_ready", "pool_passed", "dve_passed", "xres_stored", "xm_sent", "counts_link")}

        block = ctx.enter_context(nc.Block())


        @block.sync
        def _(sp):
            sp.dma_start(x_in[:, 0], io["x"][0]).then_inc(s["x_loaded"], 16)
            w_stage = decay[:].rearrange("p a b c d -> p (a b c d)")[:, 0:KD * PROJ]\
                .rearrange("p (k n) -> p k n", k=KD)
            sp.dma_start(w_stage, io["in_w"]).then_inc(s["weights_in"], 16)
            for dst, src in ((nm_w, "nm_w"), (conv_w, "conv_w"), (conv_b, "conv_b"), (d_col, "d_col"),
                             (ssm_w, "ssm_w"), (moe_w, "moe_w"), (gate_w, "gate_w")):
                sp.dma_start(dst[:], io[src]).then_inc(s["small_in"], 16)
            for dst, src in ((dt_bias, "dt_bias"), (a_log, "a_log")):
                for c in range(CH):
                    sp.dma_start(dst[:, c, :], io[src].partition_broadcast(P)).then_inc(s["small_in"], 16)
            sp.dma_start(w_out[:], io["out_w"]).then_inc(s["small_in"], 16)

            def project(g, j):
                sp.wait_ge(s["xbc_ready"], KC * g + 1)
                sp.dma_start(c_low[:, j], xbc[NS:2 * NS, j, KC - 1, :]).then_inc(s["c_moved"], 16)

            def scan(g, j, tail, more):
                if more:
                    wait(sp, s["xres_ready"], CH * g)
                    sp.dma_start(x_in[:, 1 - j], io["x"][g + 1]).then_inc(s["x_loaded"], 16)
                if tail:
                    store(g - 1, 1 - j)
                if more:
                    project(g + 1, 1 - j)

            def store(g, j):
                wait(sp, s["xres_stored"], 16 * g)
                sp.wait_ge(s["xres_ready"], CH * (g + 1))
                sp.dma_start(dram["x_res"][g], x_res[:, j]).then_inc(s["xres_stored"], 16)

            project(0, 0)
            scan(0, 0, False, True)
            with sp.Fori(0, (NG - 2) // 2) as b:
                scan(2 * b + 1, 1, True, True)
                scan(2 * b + 2, 0, True, True)
            scan(NG - 1, (NG - 1) % 2, True, False)
            store(NG - 1, (NG - 1) % 2)
            sp.wait_ge(s["xres_stored"], 16 * NG)
            sp.wait_ge(s["c_moved"], 16 * NG)

        @block.gpsimd
        def _(pool):
            passed = Pass(pool, s["pool_passed"])
            nc.gpsimd.iota(iota_e[:], pattern=[[1, NE]], base=0, channel_multiplier=0,
                           allow_small_or_imprecise_dtypes=True).then_inc(s["iota_ready"], 1)
            nc.gpsimd.iota(base_e[:], pattern=[[REGION, NE]], base=0, channel_multiplier=0,
                           allow_small_or_imprecise_dtypes=True).then_inc(s["iota_ready"], 1)

            def fill_norm(g, j):
                pool.wait_ge(s["ms_ready"], g + 1)
                nc.gpsimd.tensor_tensor(stat[:, 2, :], stat[:, 1, :], half[:], ALU.pow)\
                    .then_inc(s["rs_ready"], 1)

            def fill_seg(g, j, c):
                pool.wait_ge(s["la_ready"], g + 1)
                wait(pool, s["seg_ps"], 2 * CH * g + 2 * c)
                nc.gpsimd.tensor_tensor(la_t[:], bcast(la[:, c * NH:(c + 1) * NH], 2, P),
                                        bcast(le[:], 1, NH), ALU.mult).then_inc(s["lat_ready"], 1)

            def tail_norm(q):
                pool.wait_ge(s["ms2_ready"], q + 1)
                nc.gpsimd.tensor_tensor(tail_stat[:, 1:2], tail_stat[:, 0:1], half[:, 0:1], ALU.pow)\
                    .then_inc(s["rs2_ready"], 1)

            def tail_norm3(q):
                pool.wait_ge(s["ms3_ready"], q + 1)
                nc.gpsimd.tensor_tensor(tail_stat[:, 4:5], tail_stat[:, 3:4], half[:, 0:1], ALU.pow)\
                    .then_inc(s["rs3_ready"], 1)

            def send(g, j, chunks):
                if chunks[0] == 0:
                    pool.wait_ge(s["rows_ready"], g + 1)
                    wait(pool, s["xm_sent"], 16 * 2 * CH * g)
                    passed()
                for c in chunks:
                    for k in range(2):
                        n = 2 * c + k
                        nc.gpsimd.indirect_dma_start(
                            out=dram["sent"], out_offset=bass.IndirectOffsetOnAxis(ap=row_u[:, j, n:n + 1], axis=0),
                            in_=xm[:, j, c, :], in_offset=None).then_inc(s["xm_sent"], 16)

            def chunk(g, j, c, t, q):
                if c == 0 and j == 0:
                    wait(pool, s["inter_done"], q)
                    wait(pool, s["state_ready"], q)
                    passed()
                    nc.gpsimd.memset(state[:], 0.0).then_inc(s["state_zero"], 1)
                    pool.wait_ge(s["state_zero"], zeroed(g))
                if t:
                    tail_norm(q - 1)
                pool.wait_ge(s["xdt_ready"], q + 1)
                pool.wait_ge(s["pex_ready"], g + 1)
                nc.gpsimd.tensor_tensor(x_end[:], x_dt[:], bcast(pex[:, j, 1, c * NH:(c + 1) * NH], 2, HD),
                                        ALU.mult).then_inc(s["xend_ready"], 1)
                wait(pool, s["state_ready"], q)
                nc.gpsimd.tensor_tensor(state_p[:], state[:], bcast(pex[0:NS, j, 2, c * NH:(c + 1) * NH], 2, HD),
                                        ALU.mult).then_inc(s["statep_ready"], 1)

            def zeroed(g):
                return g // 2 + 1 if isinstance(g, int) else zero_index[0]

            zero_index = [None]

            def scan(g, j, tail, more):
                f = lambda fn, *a: fn(g + 1, 1 - j, *a) if more else None
                for c in range(CH):
                    q = CH * g + c
                    t = tail or c > 0
                    chunk(g, j, c, t, q)
                    if t:
                        tail_norm3(q - 1)
                    if c == 0:
                        f(fill_norm)
                    if c == 1:
                        f(fill_seg, 0)
                        f(fill_seg, 1)
                    if c == 2:
                        f(fill_seg, 2)
                        f(fill_seg, 3)
                        if tail:
                            send(g - 1, 1 - j, (0, 1))
                    if c == 3 and tail:
                        send(g - 1, 1 - j, (2, 3))

            fill_norm(0, 0)
            for i in range(CH):
                fill_seg(0, 0, i)
            scan(0, 0, False, True)
            with pool.Fori(0, (NG - 2) // 2) as b:
                zero_index[0] = b + 2
                passed.times = (NG - 2) // 2
                scan(2 * b + 1, 1, True, True)
                scan(2 * b + 2, 0, True, True)
                passed.times = 1
            scan(NG - 1, (NG - 1) % 2, True, False)
            tail_norm(CH * NG - 1)
            tail_norm3(CH * NG - 1)
            send(NG - 1, (NG - 1) % 2, (0, 1, 2, 3))
            pool.wait_ge(s["xm_sent"], 16 * 2 * CH * NG)
            passed.done()

        @block.scalar
        def _(act):
            act.wait_ge(s["a_exp"], 1)
            nc.scalar.activation(a_neg[:], a_neg[:], ACT.Exp).then_inc(s["a_exp"], 1)

            def norm_sums(g, j):
                act.wait_ge(s["x_loaded"], 16 * (g + 1))
                wait(act, s["ms_ready"], g)
                wait(act, s["ss_ready"], CH * g)
                for c in range(CH):
                    nc.scalar.activation(squares[:, c], x_in[:, j, c, :], ACT.Square,
                                         accum_out=stat[:, 0, c:c + 1]).then_inc(s["ss_ready"], 1)

            def h_parts(g, j):
                for k in range(KD):
                    act.wait_ge(s["ht_ps"], KD * g + k + 1)
                    nc.scalar.activation(h_hi[:, k], proj_ps[k][:], ACT.Copy, scale=nm_w[:, k:k + 1])\
                        .then_inc(s["h_hi_ready"], 1)

            def softplus(g, j):
                act.wait_ge(s["soft_in"], g + 1)
                nc.scalar.activation(soft[:, 2], soft[:, 1], ACT.Exp).then_inc(s["soft_exp"], 1)
                act.wait_ge(s["soft_exp"], 2 * g + 1)
                nc.scalar.activation(soft[:, 3], soft[:, 2], ACT.Ln, bias=1.0).then_inc(s["soft_exp"], 1)

            def sums_exp(g, j):
                act.wait_ge(s["cum_done"], g + 1)
                nc.scalar.activation(flat(pex[:, j]), cum_ps, ACT.Exp).then_inc(s["pex_ready"], 1)

            def seg_exp(g, j, c):
                for h in range(2):
                    n = 2 * c + h
                    act.wait_ge(s["seg_ps"], 2 * CH * g + n + 1)
                    nc.scalar.activation(flat(decay[:, j, c])[:, h * GT:(h + 1) * GT], proj_ps[n % 2][:], ACT.Exp)\
                        .then_inc(s["decay_ready"], 1)

            def tile_out(g, j, i):
                act.wait_ge(s["tile_ps"], TILES * g + i + 1)
                if i < KC:
                    k = (i + KC - 1) % KC
                    wait(act, s["conv_ready"], KC * g)
                    nc.scalar.activation(raw[:, j, k, TAPS - 1:], proj_ps[i % 2][:], ACT.Identity)\
                        .then_inc(s["tile_out"], 1)
                else:
                    nc.scalar.activation(z_act[:, j, i - KC, :], proj_ps[i % 2][:], ACT.Silu)\
                        .then_inc(s["tile_out"], 1)

            def conv_out(g, j, n):
                k = (n + KC - 1) % KC
                act.wait_ge(s["conv_ready"], KC * g + n + 1)
                nc.scalar.activation(xbc[:, j, k, :], conv[:, n % 2, :], ACT.Silu)\
                    .then_inc(s["xbc_ready"], 1)

            def tail_square(q):
                act.wait_ge(s["h1_ready"], q + 1)
                wait(act, s["ms3_ready"], q)
                wait(act, s["ss3_ready"], q)
                nc.scalar.activation(tail_squares[:], h1[:], ACT.Square, accum_out=tail_stat[:, 2:3])\
                    .then_inc(s["ss3_ready"], 1)

            def tail_xmt(q):
                act.wait_ge(s["xmt_done"], q + 1)
                wait(act, s["logit_done"], q)
                for k in range(KD):
                    nc.scalar.activation(xm_t[:, k], xmt_ps[:, k * P:(k + 1) * P], ACT.Copy,
                                         scale=moe_w[:, k:k + 1]).then_inc(s["xmt_ready"], 1)

            def scan(g, j, tail, more):
                f = lambda fn, *a: fn(g + 1, 1 - j, *a) if more else None
                for c in range(CH):
                    q = CH * g + c
                    t = tail or c > 0
                    if t:
                        tail_square(q - 1)
                    if c == 2:
                        f(seg_exp, 1)
                        f(seg_exp, 2)
                    if c == 3:
                        f(tile_out, 3)
                        f(conv_out, 1)
                    if t:
                        tail_xmt(q - 1)
                    if c == 0:
                        f(norm_sums)
                    if c == 1:
                        f(softplus)
                    if c == 2:
                        f(seg_exp, 3)
                        f(tile_out, 0)
                    if c == 3:
                        f(tile_out, 4)
                        f(tile_out, 5)
                        f(conv_out, 2)
                    act.wait_ge(s["yg_ready"], q + 1)
                    nc.scalar.activation(y_sq[:], y_gated[:], ACT.Square).then_inc(s["ysq_ready"], 1)
                    if c == 0:
                        f(h_parts)
                    if c == 1:
                        f(sums_exp)
                        f(seg_exp, 0)
                    if c == 2:
                        f(tile_out, 1)
                        f(tile_out, 2)
                        f(conv_out, 0)
                    if c == 3:
                        f(tile_out, 6)
                        f(conv_out, 3)
                        f(tile_out, 7)
                        f(tile_out, 8)
                        f(conv_out, 4)

            act.wait_ge(s["small_in"], 16 * SMALL_DMAS)
            norm_sums(0, 0)
            h_parts(0, 0)
            softplus(0, 0)
            sums_exp(0, 0)
            for i in range(CH):
                seg_exp(0, 0, i)
            for i in range(TILES):
                tile_out(0, 0, i)
                if 1 <= i <= KC:
                    conv_out(0, 0, i - 1)
            scan(0, 0, False, True)
            with act.Fori(0, (NG - 2) // 2) as b:
                scan(2 * b + 1, 1, True, True)
                scan(2 * b + 2, 0, True, True)
            scan(NG - 1, (NG - 1) % 2, True, False)
            tail_square(CH * NG - 1)
            tail_xmt(CH * NG - 1)

        @block.tensor
        def _(pe):
            mm = nc.tensor.matmul

            def split_mm(out, a_hi, a_lo, b_hi, b_lo, first, last):
                mm(out, a_hi, b_hi, start=first, stop=False)
                mm(out, a_hi, b_lo, start=False, stop=False)
                return mm(out, a_lo, b_hi, start=False, stop=last)

            def transposes(g, j):
                for k in range(KD):
                    wait(pe, s["tile_out"], TILES * g)
                    for c in range(CH):
                        if k == 0:
                            pe.wait_ge(s["xn_ready"], CH * g + c + 1)
                        i = nc.tensor.transpose(proj_ps[k][:, c * P:(c + 1) * P],
                                                x_norm[:, c, k * P:(k + 1) * P], ident[:])
                    i.then_inc(s["ht_ps"], 1)

            def dt_proj(g, j):
                pe.wait_ge(s["h_lo_ready"], KD * (g + 1))
                if isinstance(g, int) and g == 0:
                    pe.wait_ge(s["w_split"], 4)
                for c in range(CH):
                    for k in range(KD):
                        t = slice(c * P, (c + 1) * P)
                        i = split_mm(dt_ps[:, c * NH:(c + 1) * NH], h_hi[:, k, t], h_lo[:, k, t],
                                     w_hi[:, k, COL_DT:], w_lo[:, k, COL_DT:], k == 0, k == KD - 1)
                i.then_inc(s["dt_done"], 1)

            def sums(g, j):
                pe.wait_ge(s["la_ready"], g + 1)
                for n, m in enumerate((le, gt, ones)):
                    i = mm(cum_ps[:, 32 * n:32 * n + 32], m[:], la[:], start=True, stop=True)
                i.then_inc(s["cum_done"], 1)

            def seg(g, j, c):
                pe.wait_ge(s["lat_ready"], CH * g + c + 1)
                for h in range(2):
                    n = 2 * c + h
                    if n == 0:
                        pe.wait_ge(s["pex_ready"], g + 1)
                    elif n == 1:
                        pe.wait_ge(s["h_lo_ready"], KD * (g + 1))
                        wait(pe, s["rows_ready"], g - 1 if not isinstance(g, int) else max(g - 1, 0))
                    else:
                        pe.wait_ge(s["decay_ready"], 2 * CH * g + n - 1)
                    mm(proj_ps[n % 2][:], gt[:], flat(la_t[:])[:, h * GT:(h + 1) * GT], start=True, stop=True)\
                        .then_inc(s["seg_ps"], 1)

            def tile(g, j, i):
                if i < 2:
                    pe.wait_ge(s["decay_ready"], 2 * CH * (g + 1) - 1 + i)
                else:
                    pe.wait_ge(s["tile_out"], TILES * g + i - 1)
                col = COL_BC if i == 0 else COL_X + (i - 1) * P if i < KC else (i - KC) * P
                for k in range(KD):
                    r = split_mm(proj_ps[i % 2][:], w_hi[:, k, col:col + P], w_lo[:, k, col:col + P],
                                 h_hi[:, k, :], h_lo[:, k, :], k == 0, k == KD - 1)
                r.then_inc(s["tile_ps"], 1)

            def s1(g, j, c, q):
                if c == 0:
                    pe.wait_ge(s["xbc_ready"], KC * (g + 1))
                    pe.wait_ge(s["c_moved"], 16 * (g + 1))
                t = slice(c * P, (c + 1) * P)
                wait(pe, s["state_ready"], q)
                wait(pe, s["b_ready"], q)
                for k in range(KI):
                    nc.tensor.transpose(x_ps[:, k * P:(k + 1) * P], xbc[:, j, k, t], ident[:])
                nc.tensor.transpose(bt_ps, xbc[:, j, KC - 1, t], ident[:])
                wait(pe, s["cb_ready"], q)
                mm(cb_ps, xbc[0:NS, j, KC - 1, t], c_low[:, j, t], start=True, stop=True)\
                    .then_inc(s["s1_done"], 1)
                if c == 0 and j == 0:
                    pe.wait_ge(s["state_zero"], g // 2 + 1 if isinstance(g, int) else zero_index[0])
                wait(pe, s["yin_ready"], q)
                mm(inter_ps[:], c_low[:, j, t], flat(state[:]), start=True, stop=True)\
                    .then_inc(s["inter_done"], 1)

            def s3(g, j, c, q):
                pe.wait_ge(s["m_ready"], q + 1)
                pe.wait_ge(s["xdt_ready"], q + 1)
                wait(pe, s["ytok_ready"], q)
                for h in range(NH):
                    i = mm(intra_ps[:, h * HD:(h + 1) * HD], decay[:, j, c, h, :], x_dt[:, h, :],
                           start=True, stop=True)
                i.then_inc(s["intra_done"], 1)
                pe.wait_ge(s["xend_ready"], q + 1)
                pe.wait_ge(s["b_ready"], q + 1)
                mm(x_ps[0:NS, :], b_tok[:], flat(x_end[:]), start=True, stop=True).then_inc(s["state_done"], 1)

            def s5(q):
                pe.wait_ge(s["ytok_ready"], q + 1)
                wait(pe, s["yd_ready"], KI * q)
                for k in range(KI):
                    i = nc.tensor.transpose(yt_ps[:, k * P:(k + 1) * P], flat(y_tok[:])[:, k * P:(k + 1) * P], ident[:])
                i.then_inc(s["yt_done"], 1)

            def s6(q):
                pe.wait_ge(s["yg_ready"], q + 1)
                pe.wait_ge(s["ysq_ready"], q + 1)
                wait(pe, s["logit_ready"], q)
                for k in range(KI):
                    mm(out_ps, y_gated[:, k, :], w_out[:, k, :], start=k == 0, stop=k == KI - 1)
                for k in range(KI):
                    i = mm(ss_ps, y_sq[:, k, :], ones[:, 0:1], start=k == 0, stop=k == KI - 1)
                i.then_inc(s["out_done"], 1)

            def tail_t(q):
                pe.wait_ge(s["xm_ready"], q + 1)
                wait(pe, s["xmt_ready"], KD * q)
                for k in range(KD):
                    c = tail_chunk[0]
                    i = nc.tensor.transpose(xmt_ps[:, k * P:(k + 1) * P],
                                            xm[:, tail_parity[0], c, k * P:(k + 1) * P], ident[:])
                i.then_inc(s["xmt_done"], 1)

            def tail_logits(q):
                pe.wait_ge(s["xmt_ready"], KD * (q + 1))
                wait(pe, s["logit_ready"], q)
                for k in range(KD):
                    i = mm(logit_ps, xm_t[:, k], gate_w[:, k], start=k == 0, stop=k == KD - 1)
                i.then_inc(s["logit_done"], 1)

            def ranks(g, more):
                pe.wait_ge(s["hot_ready"], g + 1)
                if not more:
                    pe.wait_ge(s["tile_out"], TILES * NG)
                    pe.wait_ge(s["rows_ready"], g)
                mm(rank_ps[:, 0:32], lt[:], flat(hot[:, 2]), start=True, stop=True)
                mm(rank_ps[:, 32:64], ones[:], flat(hot[:, 2]), start=True, stop=True).then_inc(s["rank_done"], 1)

            tail_chunk, tail_parity, zero_index = [0], [0], [None]

            def scan(g, j, tail, more):
                f = lambda fn, *a: fn(g + 1, 1 - j, *a) if more else None
                for c in range(CH):
                    q = CH * g + c
                    t = tail or c > 0
                    tail_chunk[0], tail_parity[0] = (c - 1) % CH, j if c else 1 - j
                    s1(g, j, c, q)
                    if c == 1:
                        f(dt_proj)
                        if tail:
                            ranks(g - 1, more)
                    if c == 2:
                        f(seg, 1)
                        f(seg, 2)
                    if c == 3:
                        f(tile, 3)
                    s3(g, j, c, q)
                    if t:
                        tail_t(q - 1)
                    if c == 2:
                        f(seg, 3)
                        f(tile, 0)
                    if c == 3:
                        f(tile, 4)
                        f(tile, 5)
                    s5(q)
                    if t:
                        tail_logits(q - 1)
                    if c == 1:
                        f(sums)
                    if c == 2:
                        f(tile, 1)
                    if c == 3:
                        f(tile, 6)
                    s6(q)
                    if c == 0:
                        f(transposes)
                    if c == 1:
                        f(seg, 0)
                    if c == 2:
                        f(tile, 2)
                    if c == 3:
                        f(tile, 7)
                        f(tile, 8)

            transposes(0, 0)
            dt_proj(0, 0)
            sums(0, 0)
            for i in range(CH):
                seg(0, 0, i)
            for i in range(TILES):
                tile(0, 0, i)
            pe.wait_ge(s["w_scaled"], 1)
            scan(0, 0, False, True)
            with pe.Fori(0, (NG - 2) // 2) as b:
                zero_index[0] = b + 2
                scan(2 * b + 1, 1, True, True)
                scan(2 * b + 2, 0, True, True)
            scan(NG - 1, (NG - 1) % 2, True, False)
            tail_chunk[0], tail_parity[0] = CH - 1, (NG - 1) % 2
            tail_t(CH * NG - 1)
            tail_logits(CH * NG - 1)
            ranks(NG - 1, False)

        @block.vector
        def _(dve):
            passed = Pass(dve, s["dve_passed"])
            tt, stt, ts = nc.vector.tensor_tensor, nc.vector.scalar_tensor_tensor, nc.vector.tensor_scalar
            dve.wait_ge(s["small_in"], 16 * SMALL_DMAS)
            ts(a_neg[:], a_log[:], A_LOG_MAX, None, ALU.min).then_inc(s["a_exp"], 1)
            nc.vector.memset(raw[:, 0, :, 0:TAPS - 1], 0.0).then_inc(s["halo_ready"], 1)
            dve.wait_ge(s["iota_ready"], 2)
            nc.vector.tensor_copy(run[:, 0, :], base_e[:]).then_inc(s["counts_link"], 1)
            for k in range(KI):
                i = ts(w_out[:, k, :], w_out[:, k, :], ssm_w[:, k:k + 1], None, ALU.mult)
            i.then_inc(s["w_scaled"], 1)
            dve.wait_ge(s["a_exp"], 2)
            ts(a_neg[:], a_neg[:], -1.0, None, ALU.mult).then_inc(s["a_ready"], 1)
            w_stage = decay[:].rearrange("p a b c d -> p (a b c d)")[:, 0:KD * PROJ]\
                .rearrange("p (k n) -> p k n", k=KD)
            dve.wait_ge(s["weights_in"], 16)
            for k in range(KD):
                nc.vector.tensor_copy(w_hi[:, k], w_stage[:, k]).then_inc(s["w_split"], 1)
            for k in range(KD):
                dve.wait_ge(s["w_split"], k + 1)
                tt(w_lo[:, k], w_stage[:, k], w_hi[:, k].bitcast(F32), ALU.subtract)\
                    .then_inc(s["w_split"], 1)

            def norm(g, j):
                dve.wait_ge(s["ss_ready"], CH * (g + 1))
                ts(stat[:, 1, :], stat[:, 0, :], 1.0 / D, RMS_EPS, ALU.mult, ALU.add)\
                    .then_inc(s["ms_ready"], 1)
                dve.wait_ge(s["rs_ready"], g + 1)
                wait(dve, s["ht_ps"], KD * g)
                for c in range(CH):
                    ts(x_norm[:, c, :], x_in[:, j, c, :], stat[:, 2, c:c + 1], None, ALU.mult)\
                        .then_inc(s["xn_ready"], 1)

            def h_parts(g, j):
                for k in range(KD):
                    dve.wait_ge(s["h_hi_ready"], KD * g + k + 1)
                    stt(h_lo[:, k], proj_ps[k][:], nm_w[:, k:k + 1], h_hi[:, k].bitcast(F32),
                        ALU.mult, ALU.subtract).then_inc(s["h_lo_ready"], 1)

            def softplus(g, j):
                link = Link(dve, s["soft_link"], SOFT_LINKS * g)
                v, u, ln = soft[:, 0], soft[:, 2], soft[:, 3]
                p, m, d = soft[:, 4], soft[:, 5], soft[:, 6]
                dve.wait_ge(s["dt_done"], g + 1)
                link(tt(v, dt_ps, flat(dt_bias[:]), ALU.add))
                stt(soft[:, 1], v, -1.0, v, ALU.mult, ALU.min).then_inc(s["soft_in"], 1)
                dve.wait_ge(s["soft_exp"], 2 * (g + 1))
                link(ts(p, u, -0.25, 1.0 / 3, ALU.mult, ALU.add))
                link(tt(d, p, u, ALU.mult))
                link(stt(p, d, -0.5, u, ALU.add, ALU.mult))
                link(stt(d, p, 1.0, u, ALU.add, ALU.mult))
                link(tt(p, d, ln, ALU.subtract))
                link(ts(m, u, SMALL, None, ALU.is_lt))
                link(tt(d, p, m, ALU.mult))
                link(tt(p, d, ln, ALU.add))
                link(stt(dt[:, j], v, 0.0, p, ALU.max, ALU.add))
                link(tt(m, dt[:, j], flat(a_neg[:]), ALU.mult))
                if not (isinstance(g, int) and g == 0):
                    dve.wait_ge(s["pex_ready"], g)
                    dve.wait_ge(s["seg_ps"], 2 * CH * g)
                ts(la[:], m, DECAY_MIN, None, ALU.max).then_inc(s["la_ready"], 1)
                assert link.n == SOFT_LINKS

            def convolve(g, j, i):
                k = (i + KC - 1) % KC
                n = KC * g + i
                dve.wait_ge(s["tile_out"], TILES * g + i + 1)
                if i == 0 and j == 1:
                    nc.vector.tensor_copy(raw[:, 1, :, 0:TAPS - 1], raw[:, 0, :, GT:])\
                        .then_inc(s["halo_ready"], 1)
                    dve.wait_ge(s["halo_ready"], halo(g))
                wait(dve, s["xbc_ready"], n - 1 if i > 0 or not isinstance(g, int) else max(n - 1, 0))
                link = Link(dve, s["conv_link"], (TAPS - 1) * n)
                acc = conv[:, i % 2, :]
                link(ts(acc, raw[:, j, k, TAPS - 1:], conv_w[:, k, TAPS - 1:], conv_b[:, k:k + 1],
                        ALU.mult, ALU.add))
                for m in range(TAPS - 1):
                    r = stt(acc, raw[:, j, k, m:m + GT], conv_w[:, k, m:m + 1], acc, ALU.mult, ALU.add)
                    if m < TAPS - 2:
                        link(r)
                r.then_inc(s["conv_ready"], 1)

            def halo(g):
                return (g + 1) // 2 + 1 if isinstance(g, int) else halo_index[0]

            halo_index = [None]

            def front(g, j, c, q):
                dve.wait_ge(s["s1_done"], q + 1)
                tt(cb[:], cb_ps, le[:], ALU.mult).then_inc(s["cb_ready"], 1)
                nc.vector.tensor_copy(b_tok[:], bt_ps[:, 0:NS]).then_inc(s["b_ready"], 1)
                tt(x_dt[:], x_ps[:].rearrange("p (h d) -> p h d", h=NH),
                   bcast(dt[:, j, c * NH:(c + 1) * NH], 2, HD), ALU.mult).then_inc(s["xdt_ready"], 1)

            def weigh(g, j, c, q):
                dve.wait_ge(s["decay_ready"], 2 * CH * g + 2 * c + 2)
                dve.wait_ge(s["cb_ready"], q + 1)
                tt(decay[:, j, c], decay[:, j, c], bcast(cb[:], 1, NH), ALU.mult).then_inc(s["m_ready"], 1)

            def earlier(g):
                return max(g - 1, 0) if isinstance(g, int) else g - 1

            def tail_a(q):
                dve.wait_ge(s["out_done"], q + 1)
                ts(tail_stat[:, 0:1], ss_ps, 1.0 / DI, RMS_EPS, ALU.mult, ALU.add)\
                    .then_inc(s["ms2_ready"], 1)

            def tail_b(g, j, c, q):
                dve.wait_ge(s["rs2_ready"], q + 1)
                wait(dve, s["ss3_ready"], q)
                stt(h1[:], out_ps, tail_stat[:, 1:2], x_in[:, j, c, :], ALU.mult, ALU.add)\
                    .then_inc(s["h1_ready"], 1)
                dve.wait_ge(s["h1_ready"], q + 1)
                if c == 0:
                    wait(dve, s["xres_stored"], 16 * earlier(g))
                tt(x_res[:, j, c, :], h1[:], x_in[:, j, c, :], ALU.add).then_inc(s["xres_ready"], 1)

            def tail_c(g, j, c, q):
                dve.wait_ge(s["ss3_ready"], q + 1)
                ts(tail_stat[:, 3:4], tail_stat[:, 2:3], 1.0 / D, RMS_EPS, ALU.mult, ALU.add)\
                    .then_inc(s["ms3_ready"], 1)
                dve.wait_ge(s["rs3_ready"], q + 1)
                if c == 0:
                    wait(dve, s["xm_sent"], 16 * 2 * CH * earlier(g))
                ts(xm[:, j, c, :], h1[:], tail_stat[:, 4:5], None, ALU.mult).then_inc(s["xm_ready"], 1)

            def middle(g, j, c, q):
                dve.wait_ge(s["inter_done"], q + 1)
                wait(dve, s["ytok_ready"], q)
                tt(y_in[:], inter_ps[:].rearrange("p (h d) -> p h d", h=NH),
                   bcast(pex[:, j, 0, c * NH:(c + 1) * NH], 2, HD), ALU.mult).then_inc(s["yin_ready"], 1)
                dve.wait_ge(s["intra_done"], q + 1)
                dve.wait_ge(s["yin_ready"], q + 1)
                wait(dve, s["yt_done"], q)
                tt(y_tok[:], y_in[:], intra_ps[:].rearrange("p (h d) -> p h d", h=NH), ALU.add)\
                    .then_inc(s["ytok_ready"], 1)
                dve.wait_ge(s["statep_ready"], q + 1)
                dve.wait_ge(s["state_done"], q + 1)
                tt(state[:], state_p[:], x_ps[0:NS, :].rearrange("p (h d) -> p h d", h=NH), ALU.add)\
                    .then_inc(s["state_ready"], 1)

            def gate(g, j, c, q):
                t = slice(c * P, (c + 1) * P)
                dve.wait_ge(s["yt_done"], q + 1)
                wait(dve, s["yg_ready"], q)
                for k in range(KI):
                    stt(y_d[:, k, :], xbc[:, j, k, t], d_col[:, k:k + 1], yt_ps[:, k * P:(k + 1) * P],
                        ALU.mult, ALU.add).then_inc(s["yd_ready"], 1)
                dve.wait_ge(s["yd_ready"], KI * (q + 1))
                wait(dve, s["out_done"], q)
                if c == 0:
                    dve.wait_ge(s["tile_out"], TILES * (g + 1))
                tt(y_gated[:], y_d[:], z_act[:, j, :, t], ALU.mult).then_inc(s["yg_ready"], 1)

            def tail_d(g, c, q):
                dve.wait_ge(s["logit_done"], q + 1)
                nc.vector.tensor_copy(logits[:, c, :], logit_ps).then_inc(s["logit_ready"], 1)

            def route_a(g):
                link = Link(dve, s["route_link"], ROUTE_LINKS * g)
                dve.wait_ge(s["logit_ready"], CH * (g + 1))
                passed()
                for c in range(CH):
                    r = nc.vector.max(top[:, c, :], logits[:, c, :])
                link(r, passed)
                for c in range(CH):
                    r = nc.vector.max_index(top_i[:, c, :], top[:, c, :], logits[:, c, :])
                link(r)
                link(nc.vector.tensor_copy(top_f[:], top_i[:]))
                for k in range(2):
                    r = tt(hot[:, k], bcast(iota_e[:], 1, CH), top_f[:, :, k:k + 1].to_broadcast([P, CH, NE]),
                           ALU.is_equal)
                link(r)
                tt(hot[:, 2], hot[:, 0], hot[:, 1], ALU.add).then_inc(s["hot_ready"], 1)
                link(tt(gap_all[:, bass.ds(CH * g, CH)], top[:, :, 1], top[:, :, 0], ALU.subtract))
                return link

            def route_b(g, j, link):
                dve.wait_ge(s["rank_done"], g + 1)
                for c in range(CH):
                    link(tt(run[:, c + 1, :], run[:, c, :], rank_ps[:, 32 + c * NE:32 + (c + 1) * NE], ALU.add))
                link(tt(rank[:], run[:, 0:CH, :], rank_ps[:, 0:32].rearrange("p (c e) -> p c e", c=CH), ALU.add))
                for k in range(2):
                    r = tt(picked[:, k], rank[:], hot[:, k], ALU.mult)
                link(r)
                for k in range(2):
                    r = nc.vector.tensor_reduce(row_f[:, :, k], picked[:, k], AX.X, ALU.add)
                link(r)
                nc.vector.tensor_copy(row_u[:, j, :], flat(row_f[:]))\
                    .then_inc(s["rows_ready"], 1)
                link(nc.vector.tensor_copy(rows_all[:, bass.ds(2 * CH * g, 2 * CH)],
                                           flat(row_f[:])))
                link(nc.vector.tensor_copy(run[:, 0, :], run[:, CH, :]))
                assert link.n == ROUTE_LINKS, link.n

            def scan(g, j, tail, more):
                f = lambda fn, *a: fn(g + 1, 1 - j, *a) if more else None
                for c in range(CH):
                    q = CH * g + c
                    t = tail or c > 0
                    of = (g, j, c - 1, q - 1) if c else (g - 1, 1 - j, CH - 1, q - 1)
                    if t:
                        tail_a(q - 1)
                    front(g, j, c, q)
                    if t:
                        tail_b(*of)
                    weigh(g, j, c, q)
                    if t:
                        tail_c(*of)
                    if c == 1:
                        f(softplus)
                        if tail:
                            route_b(g - 1, 1 - j, links[0])
                    if c == 3:
                        f(convolve, 2)
                    middle(g, j, c, q)
                    if c == 3:
                        f(convolve, 3)
                    gate(g, j, c, q)
                    if t:
                        tail_d(of[0], of[2], q - 1)
                    if c == 0:
                        f(norm)
                        if tail:
                            links[0] = route_a(g - 1)
                        f(h_parts)
                    if c == 2:
                        f(convolve, 0)
                        f(convolve, 1)
                    if c == 3:
                        f(convolve, 4)

            links = [None]
            norm(0, 0)
            h_parts(0, 0)
            dve.wait_ge(s["a_ready"], 1)
            softplus(0, 0)
            for i in range(KC):
                convolve(0, 0, i)
            scan(0, 0, False, True)
            with dve.Fori(0, (NG - 2) // 2) as b:
                halo_index[0] = b + 3
                passed.times = (NG - 2) // 2
                scan(2 * b + 1, 1, True, True)
                scan(2 * b + 2, 0, True, True)
                passed.times = 1
            scan(NG - 1, (NG - 1) % 2, True, False)
            q = CH * NG - 1
            of = (NG - 1, (NG - 1) % 2, CH - 1, q)
            tail_a(q)
            tail_b(*of)
            tail_c(*of)
            tail_d(of[0], of[2], q)
            link = route_a(NG - 1)
            route_b(NG - 1, (NG - 1) % 2, link)
            table = routing["table"]
            link = Link(dve, s["counts_link"], 1)
            row = slice(0, 1)
            end, n_rows, n_items, before = run[:, 0, :], run[:, 1, :], run[:, 2, :], run[:, 3, :]
            link(nc.vector.memset(table[:], 0))
            link(nc.vector.tensor_copy(table[:, PAD_ROW:PAD_ROW + NE], end[row]))
            link(tt(n_rows, end, base_e[:], ALU.subtract))
            link(ts(n_rows, n_rows, float(ROWS - 1), None, ALU.add))
            link(nc.vector.tensor_copy(items_i[:], n_rows))
            link(ts(items_i[:], items_i[:], ROWS.bit_length() - 1, None, ALU.arith_shift_right))
            link(nc.vector.tensor_copy(table[:, ITEMS:ITEMS + NE], items_i[row, :]))
            link(nc.vector.tensor_copy(n_items, items_i[:]))
            link(ts(routing["step"][:], n_items, float(ROWS), float(-REGION), ALU.mult, ALU.add))
            for e in range(NE):
                link(tt(before[:, e:e + 1], n_items[:, e:e + 1], before[:, e - 1:e] if e else zero1[:],
                        ALU.add))
            link(nc.vector.tensor_copy(table[:, FIRST + 1:FIRST + 1 + NE], before[row, :]))
            passed.done()


def expert_phase(nc, io, dram, cst, routing):
    with ExitStack() as ctx:
        def sb(name, shape, dt=F32):
            return ctx.enter_context(nc.sbuf_tensor("e_" + name, shape, dt))

        def sem(name):
            return ctx.enter_context(nc.semaphore("e_" + name))

        ident, moe_w, table = cst["ident"], cst["moe_w"], routing["table"]
        W1, W2 = KD * FF, KF * D
        stage = sb("stage", [P, W1 + W2])
        w_hi = sb("w_hi", [P, 2, W1 + W2], F32R)
        w_lo = sb("w_lo", [P, 2, W1 + W2], F32R)
        zeros = sb("zeros", [P, RT, D])
        x_rows = sb("x_rows", [P, RT, D])
        x_hi = sb("x_hi", [P, KD, ROWS], F32R)
        x_lo = sb("x_lo", [P, KD, ROWS], F32R)
        h_act = sb("h_act", [P, 2, 2 * ROWS])
        h_hi = sb("h_hi", [P, KF, ROWS], F32R)
        h_lo = sb("h_lo", [P, KF, ROWS], F32R)
        y_rows = sb("y_rows", [P, RT, D])
        w8 = sb("w8", [P, FFN_W], I8)
        moved = sb("moved", [P, 2 * CH * NG])
        shift = sb("shift", [P, 2 * CH * NG])
        share, gap_all = routing["share"], routing["gap"]
        pairs = KF // 2
        bank = [ctx.enter_context(nc.psum_tensor(f"e_bank{i}", [P, 512], F32)) for i in range(7)]
        h_ps, xt_ps, y_ps = bank[0:pairs], bank[pairs], bank[pairs + 1:]
        s = {n: sem(n) for n in (
            "w_in", "w_split", "w_ready", "zeros_ready", "pad_filled", "x_in", "xt_done", "x_hi_ready",
            "x_lo_ready", "h_done", "h_act_ready", "h_hi_ready", "h_lo_ready", "y_done", "y_out",
            "y_stored", "pool_passed", "pe_passed", "w8_in", "share_exp", "share_link", "ffn_ready")}
        block = ctx.enter_context(nc.Block())

        def experts(eng, body):
            with eng.Fori(0, NE // 2) as pair:
                for par in range(2):
                    e = 2 * pair + par
                    items = eng.value_load(table[0:1, bass.ds(ITEMS + e, 1)], min_val=0, max_val=T // ROWS)
                    first = eng.value_load(table[0:1, bass.ds(FIRST + e, 1)], min_val=0, max_val=MAX_ITEMS)
                    body(e, par, items, first)

        @block.sync
        def _(sp):
            sp.dma_start(w8[:].bitcast(I32), io["ffn_w"]).then_inc(s["w8_in"], 16)
            sp.wait_ge(s["zeros_ready"], 1)
            for e in range(NE):
                row = sp.value_load(table[0:1, PAD_ROW + e:PAD_ROW + e + 1], min_val=e * REGION,
                                    max_val=e * REGION + T)
                sp.dma_start(dram["sent"][bass.ds(row, ROWS), :].rearrange("(r p) d -> p r d", p=P), zeros[:])\
                    .then_inc(s["pad_filled"], 16)
            for n in range(T * 2 // ROWS, MAX_ITEMS):
                sp.dma_start(dram["back"][n * ROWS:(n + 1) * ROWS, :].rearrange("(r p) d -> p r d", p=P), zeros[:])\
                    .then_inc(s["pad_filled"], 16)
            sp.wait_ge(s["pad_filled"], 16 * 2 * NE)

            def body(e, par, items, first):
                with sp.Fori(0, items) as g:
                    i = first + g
                    sp.wait_ge(s["xt_done"], i)
                    sp.dma_start(x_rows[:], dram["sent"][bass.ds(e * REGION + g * ROWS, ROWS), :]
                                 .rearrange("(r p) d -> p r d", p=P)).then_inc(s["x_in"], 16)

            experts(sp, body)
            total = sp.value_load(table[0:1, FIRST + NE:FIRST + NE + 1], min_val=0, max_val=MAX_ITEMS)
            sp.wait_ge(s["xt_done"], total)
            sp.dma_start(x_rows[:], zeros_dram_view(dram)).then_inc(s["x_in"], 16)

        @block.gpsimd
        def _(pool):
            passed = Pass(pool, s["pool_passed"])
            nc.gpsimd.memset(zeros[:], 0.0).then_inc(s["zeros_ready"], 1)
            pool.dma_start(stage[:], io["w12"][0]).then_inc(s["w_in"], 16)
            half = (W1 + W2) // 2
            passed.times = NE // 2
            with pool.Fori(0, NE // 2) as pair:
                for par in range(2):
                    e = 2 * pair + par
                    freed = pool.value_load(table[0:1, bass.ds(FIRST - 1 + e, 1)], min_val=0, max_val=MAX_ITEMS)
                    pool.wait_ge(s["y_done"], freed)
                    pool.wait_ge(s["w_in"], 16 * (e + 1))
                    passed()
                    for n in range(2):
                        t = slice(n * half, (n + 1) * half)
                        nc.gpsimd.tensor_copy(w_hi[:, par, t], stage[:, t]).then_inc(s["w_split"], 1)
                        pool.wait_ge(s["w_split"], 2 * e + n + 1)
                        nc.gpsimd.tensor_tensor(w_lo[:, par, t], stage[:, t], w_hi[:, par, t].bitcast(F32),
                                                ALU.subtract).then_inc(s["w_ready"], 1)
                    if par == 0:
                        pool.wait_ge(s["w_ready"], 2 * (e + 1))
                        pool.dma_start(stage[:], io["w12"][e + 1]).then_inc(s["w_in"], 16)
                    else:
                        nxt = pool.snap((e + 1) % NE)
                        pool.wait_ge(s["w_ready"], 2 * (e + 1))
                        pool.dma_start(stage[:], io["w12"][nxt]).then_inc(s["w_in"], 16)
            pool.wait_ge(s["w_in"], 16 * (NE + 1))
            passed.done()

        @block.scalar
        def _(act):
            nc.scalar.activation(share[:, 1], gap_all[:], ACT.Exp).then_inc(s["share_exp"], 1)

            def x_parts(i):
                act.wait_ge(s["xt_done"], i + 1)
                for k in range(KD):
                    nc.scalar.activation(x_hi[:, k], xt_ps[:, k * ROWS:(k + 1) * ROWS], ACT.Copy,
                                         scale=moe_w[:, k:k + 1]).then_inc(s["x_hi_ready"], 1)

            x_parts(0)
            act.wait_ge(s["pad_filled"], 16 * 2 * NE)

            def body(e, par, items, first):
                with act.Fori(0, items) as g:
                    i = first + g
                    for p in range(pairs):
                        act.wait_ge(s["h_done"], pairs * i + p + 1)
                        act.wait_ge(s["h_lo_ready"], pairs * i + p - 1 if p else pairs * i)
                        nc.scalar.activation(h_act[:, p % 2], h_ps[p][:], ACT.Silu)\
                            .then_inc(s["h_act_ready"], 1)
                    x_parts(i + 1)
                    act.wait_ge(s["y_stored"], 16 * i)
                    act.wait_ge(s["y_done"], i + 1)
                    for r in range(RT):
                        nc.scalar.activation(y_rows[:, r, :], y_ps[r][:, 0:D], ACT.Copy).then_inc(s["y_out"], 1)
                    act.wait_ge(s["y_out"], RT * (i + 1))
                    at = nc.s_assert_within(i, 0, MAX_ITEMS - 1, skip_runtime_bounds_check_because=
                                            "two rows a token and each expert's last item padded: 39 items at most")
                    act.dma_start(dram["back"][bass.ds(at * ROWS, ROWS), :]
                                  .rearrange("(r p) d -> p r d", p=P), y_rows[:]).then_inc(s["y_stored"], 16)

            experts(act, body)
            total = act.value_load(table[0:1, FIRST + NE:FIRST + NE + 1], min_val=0, max_val=MAX_ITEMS)
            act.wait_ge(s["y_stored"], 16 * total)
            nc.scalar.activation(y_rows[:, 0, 0:1], y_rows[:, 0, 1:2], ACT.Copy)

        @block.tensor
        def _(pe):
            passed = Pass(pe, s["pe_passed"])
            passed.times = NE // 2
            mm = nc.tensor.matmul

            def transposes(i):
                pe.wait_ge(s["x_in"], 16 * (i + 1))
                for k in range(KD):
                    for r in range(RT):
                        t = nc.tensor.transpose(xt_ps[:, k * ROWS + r * P:k * ROWS + (r + 1) * P],
                                                x_rows[:, r, k * P:(k + 1) * P], ident[:])
                t.then_inc(s["xt_done"], 1)

            transposes(0)

            def body(e, par, items, first):
                pe.wait_ge(s["w_ready"], 2 * (e + 1))
                passed()
                w1h = w_hi[:, par, 0:W1].rearrange("p (k f) -> p k f", k=KD)
                w1l = w_lo[:, par, 0:W1].rearrange("p (k f) -> p k f", k=KD)
                w2h = w_hi[:, par, W1:].rearrange("p (k d) -> p k d", k=KF)
                w2l = w_lo[:, par, W1:].rearrange("p (k d) -> p k d", k=KF)
                with pe.Fori(0, items) as g:
                    i = first + g
                    pe.wait_ge(s["x_lo_ready"], KD * (i + 1))
                    for p in range(pairs):
                        pe.wait_ge(s["h_act_ready"], pairs * i)
                        for n in range(2):
                            f = 2 * p + n
                            out = h_ps[p][:, n * ROWS:(n + 1) * ROWS]
                            for k in range(KD):
                                t = slice(f * P, (f + 1) * P)
                                mm(out, w1h[:, k, t], x_hi[:, k], start=k == 0, stop=False)
                                mm(out, w1h[:, k, t], x_lo[:, k], start=False, stop=False)
                                r = mm(out, w1l[:, k, t], x_hi[:, k], start=False, stop=k == KD - 1)
                        r.then_inc(s["h_done"], 1)
                    transposes(i + 1)
                    pe.wait_ge(s["y_out"], RT * i)
                    order = [(r, p) for r in range(RT) for p in range(pairs - 1)] + [(r, pairs - 1) for r in range(RT)]
                    for r, p in order:
                        pe.wait_ge(s["h_lo_ready"], pairs * i + p + 1)
                        for k in (2 * p, 2 * p + 1):
                            t = slice(r * P, (r + 1) * P)
                            out = y_ps[r][:, 0:D]
                            mm(out, h_hi[:, k, t], w2h[:, k], start=k == 0, stop=False)
                            mm(out, h_hi[:, k, t], w2l[:, k], start=False, stop=False)
                            m = mm(out, h_lo[:, k, t], w2h[:, k], start=False, stop=k == KF - 1)
                    m.then_inc(s["y_done"], 1)

            experts(pe, body)
            passed.done()

        @block.vector
        def _(dve):
            tt, stt, ts = nc.vector.tensor_tensor, nc.vector.scalar_tensor_tensor, nc.vector.tensor_scalar
            dve.wait_ge(s["share_exp"], 1)
            link = Link(dve, s["share_link"], 0)
            link(ts(share[:, 0], share[:, 1], 1.0, None, ALU.add))
            link(nc.vector.reciprocal(share[:, 0], share[:, 0]))
            link(tt(share[:, 1], share[:, 1], share[:, 0], ALU.mult))
            rows = routing["rows"]
            for e in range(1, NE):
                link(ts(moved[:], rows[:], float(e * REGION), routing["step"][:, e - 1:e], ALU.is_ge, ALU.mult))
                link(tt(shift[:], shift[:], moved[:], ALU.add) if e > 1 else nc.vector.tensor_copy(shift[:], moved[:]))
            tt(routing["back_rows"][:], rows[:], shift[:], ALU.add).then_inc(s["ffn_ready"], 1)
            dve.wait_ge(s["w8_in"], 16)
            nc.vector.tensor_copy(cst["ffn_w"][:], w8[:]).then_inc(s["ffn_ready"], 1)

            def x_parts(i):
                dve.wait_ge(s["x_hi_ready"], KD * (i + 1))
                for k in range(KD):
                    stt(x_lo[:, k], xt_ps[:, k * ROWS:(k + 1) * ROWS], moe_w[:, k:k + 1], x_hi[:, k].bitcast(F32),
                        ALU.mult, ALU.subtract).then_inc(s["x_lo_ready"], 1)

            x_parts(0)

            def body(e, par, items, first):
                with dve.Fori(0, items) as g:
                    i = first + g
                    dve.wait_ge(s["y_done"], i)
                    for p in range(pairs):
                        n = pairs * i + p
                        dve.wait_ge(s["h_act_ready"], n + 1)
                        nc.vector.tensor_copy(flat(h_hi[:, 2 * p:2 * p + 2]), h_act[:, p % 2])\
                            .then_inc(s["h_hi_ready"], 1)
                        dve.wait_ge(s["h_hi_ready"], n + 1)
                        tt(flat(h_lo[:, 2 * p:2 * p + 2]), h_act[:, p % 2],
                           flat(h_hi[:, 2 * p:2 * p + 2]).bitcast(F32), ALU.subtract).then_inc(s["h_lo_ready"], 1)
                    x_parts(i + 1)

            experts(dve, body)


def zeros_dram_view(dram):
    return dram["sent"][0:ROWS, :].rearrange("(r p) d -> p r d", p=P)


def ffn_phase(nc, io, dram, cst, routing, out):
    with ExitStack() as ctx:
        def sb(name, shape, dt=F32):
            return ctx.enter_context(nc.sbuf_tensor("f_" + name, shape, dt))

        def sem(name):
            return ctx.enter_context(nc.semaphore("f_" + name))

        ident, half, w = cst["ident"], cst["half"], cst["ffn_w"]
        wg = w[:, 0:KD * FF].rearrange("p (k f) -> p k f", k=KD)
        wu = w[:, KD * FF:2 * KD * FF].rearrange("p (k f) -> p k f", k=KD)
        wd = w[:, 2 * KD * FF:].rearrange("p (k d) -> p k d", k=KF)
        s_gu = sb("s_gu", [P, 2, KF])
        s_down = sb("s_down", [P, D])
        row_u = sb("f_row_u", [P, 2 * CH], U32)
        back = sb("back", [P, CH, 2, D])
        res = sb("res", [P, CH, D])
        mixed = sb("mixed", [P, CH, D])
        bn = sb("bn", [P, 2, 6])
        mv = sb("mv", [P, CH, 2])
        var_e = sb("var_e", [P, CH])
        rs = sb("rs", [P, CH])
        x1 = sb("x1", [P, 2, CH, D])
        x_hi = sb("f_x_hi", [P, KD, GT], F32R)
        x_lo = sb("f_x_lo", [P, KD, GT], F32R)
        gate = sb("gate", [P, 2, GT])
        fused = sb("fused", [P, 2, GT])
        f_hi = sb("f_hi", [P, KF, GT], F32R)
        f_lo = sb("f_lo", [P, KF, GT], F32R)
        y = sb("y", [P, CH, D])
        mv2 = sb("mv2", [P, CH, 2])
        var2 = sb("var2", [P, CH])
        rs2 = sb("rs2", [P, CH])
        out_t = sb("out_t", [P, CH, D])
        rows_all, share = routing["back_rows"], routing["share"]
        bank = [ctx.enter_context(nc.psum_tensor(f"f_bank{i}", [P, 512], F32)) for i in range(8)]
        gate_ps, up_ps, xt_ps, down_ps = bank[0:2], bank[2:4], bank[4:6], bank[6:8]
        s = {n: sem(n) for n in (
            "scales_in", "rows_ready", "back_in", "res_in", "mix_link", "var_ready", "rs_ready", "x1_ready",
            "xt_done", "x_hi_ready", "x_lo_ready", "gate_done", "up_done", "gate_ready", "fused_ready",
            "f_hi_ready", "f_lo_ready", "down_done", "y_link", "y_ready", "var2_ready", "rs2_ready",
            "out_ready", "out_stored", "pool_passed", "dve_passed")}
        block = ctx.enter_context(nc.Block())
        pair_loops = (NG - 2) // 2

        @block.sync
        def _(sp):
            sp.dma_start(s_gu[:], io["s_gu"]).then_inc(s["scales_in"], 16)
            sp.dma_start(s_down[:], io["s_down"].partition_broadcast(P)).then_inc(s["scales_in"], 16)

            def fetch(g):
                wait(sp, s["x1_ready"], CH * g)
                sp.dma_start(res[:], dram["x_res"][g]).then_inc(s["res_in"], 16)

            def store(g):
                sp.wait_ge(s["out_ready"], CH * (g + 1))
                sp.dma_start(out[g], out_t[:]).then_inc(s["out_stored"], 16)

            fetch(0)
            fetch(1)
            with sp.Fori(0, 2 * pair_loops) as b:
                fetch(b + 2)
                store(b)
            store(NG - 2)
            store(NG - 1)
            sp.wait_ge(s["out_stored"], 16 * NG)

        @block.gpsimd
        def _(pool):
            passed = Pass(pool, s["pool_passed"])

            def take(g):
                pool.wait_ge(s["rows_ready"], g + 1)
                wait(pool, s["x1_ready"], CH * g)
                passed()
                for c in range(CH):
                    for k in range(2):
                        n = 2 * c + k
                        nc.gpsimd.indirect_dma_start(
                            out=back[:, c, k, :], out_offset=None, in_=dram["back"],
                            in_offset=bass.IndirectOffsetOnAxis(ap=row_u[:, n:n + 1], axis=0))\
                            .then_inc(s["back_in"], 16)

            def norm1(g):
                for c in range(CH):
                    pool.wait_ge(s["var_ready"], CH * g + c + 1)
                    nc.gpsimd.tensor_tensor(rs[:, c:c + 1], var_e[:, c:c + 1], half[:, 0:1], ALU.pow)\
                        .then_inc(s["rs_ready"], 1)

            def norm2(g):
                for c in range(CH):
                    pool.wait_ge(s["var2_ready"], CH * g + c + 1)
                    nc.gpsimd.tensor_tensor(rs2[:, c:c + 1], var2[:, c:c + 1], half[:, 0:1], ALU.pow)\
                        .then_inc(s["rs2_ready"], 1)

            take(0)
            norm1(0)
            take(1)
            norm1(1)
            with pool.Fori(0, 2 * pair_loops) as b:
                passed.times = 2 * pair_loops
                take(b + 2)
                norm2(b)
                norm1(b + 2)
            norm2(NG - 2)
            norm2(NG - 1)
            passed.done()

        @block.scalar
        def _(act):
            act.wait_ge(s["scales_in"], 32)

            def x_parts(g):
                for k in range(KD):
                    act.wait_ge(s["xt_done"], KD * g + k + 1)
                    nc.scalar.activation(x_hi[:, k], xt_ps[k][:], ACT.Copy).then_inc(s["x_hi_ready"], 1)

            def part(g, f):
                act.wait_ge(s["fused_ready"], KF * g + f + 1)
                nc.scalar.activation(f_hi[:, f], fused[:, f % 2], ACT.Copy).then_inc(s["f_hi_ready"], 1)

            def units(g):
                for f in range(KF):
                    n = KF * g + f
                    act.wait_ge(s["gate_done"], n + 1)
                    wait(act, s["fused_ready"], n - 1 if f else KF * g)
                    nc.scalar.activation(gate[:, f % 2], gate_ps[f % 2][:], ACT.Silu, scale=s_gu[:, 0, f:f + 1])\
                        .then_inc(s["gate_ready"], 1)
                    if f:
                        part(g, f - 1)
                part(g, KF - 1)

            x_parts(0)
            with act.Fori(0, NG - 1) as g:
                units(g)
                x_parts(g + 1)
            units(NG - 1)

        @block.tensor
        def _(pe):
            mm = nc.tensor.matmul

            def transposes(g, j):
                pe.wait_ge(s["x1_ready"], CH * (g + 1))
                wait(pe, s["x_lo_ready"], KD * g)
                for k in range(KD):
                    for c in range(CH):
                        i = nc.tensor.transpose(xt_ps[k][:, c * P:(c + 1) * P], x1[:, j, c, k * P:(k + 1) * P],
                                                ident[:])
                    i.then_inc(s["xt_done"], 1)

            def units(g):
                pe.wait_ge(s["x_lo_ready"], KD * (g + 1))
                for f in range(KF):
                    n = KF * g + f
                    t = slice(f * P, (f + 1) * P)
                    for w_t, ps, done, freed in ((wg, gate_ps, "gate_done", "gate_ready"),
                                                 (wu, up_ps, "up_done", "fused_ready")):
                        wait(pe, s[freed], n - 1 if f else KF * g)
                        for k in range(KD):
                            mm(ps[f % 2][:], w_t[:, k, t], x_hi[:, k], start=k == 0, stop=False)
                            i = mm(ps[f % 2][:], w_t[:, k, t], x_lo[:, k], start=False, stop=k == KD - 1)
                        i.then_inc(s[done], 1)

            def down(g):
                for c in range(CH):
                    wait(pe, s["y_ready"], CH * g)
                    o = down_ps[c // 2][:, (c % 2) * D:(c % 2 + 1) * D]
                    for k in range(KF):
                        if c == 0:
                            pe.wait_ge(s["f_lo_ready"], KF * g + k + 1)
                        t = slice(c * P, (c + 1) * P)
                        mm(o, f_hi[:, k, t], wd[:, k], start=k == 0, stop=False)
                        i = mm(o, f_lo[:, k, t], wd[:, k], start=False, stop=k == KF - 1)
                    i.then_inc(s["down_done"], 1)

            transposes(0, 0)
            units(0)
            transposes(1, 1)
            down(0)
            with pe.Fori(0, pair_loops) as b:
                for j in (1, 0):
                    g = 2 * b + 2 - j
                    units(g)
                    transposes(g + 1, 1 - j)
                    down(g)
            units(NG - 1)
            down(NG - 1)

        @block.vector
        def _(dve):
            passed = Pass(dve, s["dve_passed"])
            tt, stt, ts = nc.vector.tensor_tensor, nc.vector.scalar_tensor_tensor, nc.vector.tensor_scalar
            dve.wait_ge(s["scales_in"], 32)

            def rows(g):
                wait(dve, s["back_in"], 16 * 2 * CH * g)
                nc.vector.tensor_copy(row_u[:], rows_all[:, bass.ds(2 * CH * g, 2 * CH)])\
                    .then_inc(s["rows_ready"], 1)

            def mix(g, c):
                if c == 0:
                    dve.wait_ge(s["back_in"], 16 * 2 * CH * (g + 1))
                    dve.wait_ge(s["res_in"], 16 * (g + 1))
                link = Link(dve, s["mix_link"], MIX_LINKS * (CH * g + c))
                link(stt(mixed[:, c], back[:, c, 0], share[:, 0, bass.ds(CH * g + c, 1)], res[:, c], ALU.mult, ALU.add))
                link(stt(mixed[:, c], back[:, c, 1], share[:, 1, bass.ds(CH * g + c, 1)], mixed[:, c], ALU.mult, ALU.add))
                link(nc.vector.bn_stats(bn[:, 0], mixed[:, c]), passed)
                link(nc.vector.bn_aggr(mv[:, c], bn[:, 0]))
                ts(var_e[:, c:c + 1], mv[:, c, 1:2], LN_EPS, None, ALU.add).then_inc(s["var_ready"], 1)

            def scale1(g, j, c):
                dve.wait_ge(s["rs_ready"], CH * g + c + 1)
                ts(x1[:, j, c], mixed[:, c], mv[:, c, 0:1], rs[:, c:c + 1], ALU.subtract, ALU.mult)\
                    .then_inc(s["x1_ready"], 1)

            def x_parts(g):
                for k in range(KD):
                    dve.wait_ge(s["x_hi_ready"], KD * g + k + 1)
                    tt(x_lo[:, k], xt_ps[k][:], x_hi[:, k].bitcast(F32), ALU.subtract)\
                        .then_inc(s["x_lo_ready"], 1)

            def fuse(g, f):
                n = KF * g + f
                dve.wait_ge(s["up_done"], n + 1)
                dve.wait_ge(s["gate_ready"], n + 1)
                wait(dve, s["f_lo_ready"], n - 1 if f else KF * g)
                stt(fused[:, f % 2], up_ps[f % 2][:], s_gu[:, 1, f:f + 1], gate[:, f % 2], ALU.mult, ALU.mult)\
                    .then_inc(s["fused_ready"], 1)

            def part(g, f):
                dve.wait_ge(s["f_hi_ready"], KF * g + f + 1)
                tt(f_lo[:, f], fused[:, f % 2], f_hi[:, f].bitcast(F32), ALU.subtract)\
                    .then_inc(s["f_lo_ready"], 1)

            def finish(g, j, c):
                dve.wait_ge(s["down_done"], CH * g + c // 2 * 2 + 2)
                link = Link(dve, s["y_link"], Y_LINKS * (CH * g + c))
                link(tt(y[:, c], down_ps[c // 2][:, (c % 2) * D:(c % 2 + 1) * D], s_down[:], ALU.mult))
                tt(y[:, c], y[:, c], x1[:, j, c], ALU.add).then_inc(s["y_ready"], 1)
                dve.wait_ge(s["y_ready"], CH * g + c + 1)
                link(nc.vector.bn_stats(bn[:, 1], y[:, c]), passed)
                link(nc.vector.bn_aggr(mv2[:, c], bn[:, 1]))
                ts(var2[:, c:c + 1], mv2[:, c, 1:2], LN_EPS, None, ALU.add).then_inc(s["var2_ready"], 1)

            def scale2(g, c):
                dve.wait_ge(s["rs2_ready"], CH * g + c + 1)
                if c == 0:
                    wait(dve, s["out_stored"], 16 * g)
                ts(out_t[:, c], y[:, c], mv2[:, c, 0:1], rs2[:, c:c + 1], ALU.subtract, ALU.mult)\
                    .then_inc(s["out_ready"], 1)

            def group(g, j, before, ahead):
                if ahead:
                    rows(g + 1)
                for f in range(KF):
                    fuse(g, f)
                    if f:
                        part(g, f - 1)
                    if f < CH and before:
                        finish(g - 1, 1 - j, f)
                    if 1 <= f <= CH and before:
                        scale2(g - 1, f - 1)
                    if f >= CH and ahead:
                        mix(g + 1, f - CH)
                    if f > CH and ahead:
                        scale1(g + 1, 1 - j, f - CH - 1)
                part(g, KF - 1)
                if ahead:
                    scale1(g + 1, 1 - j, CH - 1)
                    x_parts(g + 1)

            rows(0)
            for c in range(CH):
                mix(0, c)
            for c in range(CH):
                scale1(0, 0, c)
            x_parts(0)
            group(0, 0, False, True)
            with dve.Fori(0, pair_loops) as b:
                passed.times = pair_loops
                for j in (1, 0):
                    group(2 * b + 2 - j, j, True, True)
            passed.times = 1
            group(NG - 1, 1, True, False)
            for c in range(CH):
                finish(NG - 1, 1, c)
            for c in range(CH):
                scale2(NG - 1, c)
            passed.done()


def build(nc, io, out):
    dram = {
        "sent": nc.dram_tensor("sent_rows", [NE * REGION, D], F32, kind="Internal").ap(),
        "back": nc.dram_tensor("back_rows", [MAX_ITEMS * ROWS, D], F32, kind="Internal").ap(),
        "x_res": nc.dram_tensor("x_res_dram", [NG, P, CH, D], F32, kind="Internal").ap(),
    }
    with ExitStack() as ctx:
        def sb(name, shape, dt=F32):
            return ctx.enter_context(nc.sbuf_tensor(name, shape, dt))

        cst = {n: sb(n, [P, P]) for n in ("ident", "le", "gt", "lt", "ones")}
        cst["half"] = sb("half", [P, CH])
        cst["zero1"] = sb("zero1", [P, 1])
        cst["moe_w"] = sb("moe_w", [P, KD])
        routing = {
            "rows": sb("rows_all", [P, 2 * CH * NG]),
            "back_rows": sb("back_rows_all", [P, 2 * CH * NG], U32),
            "step": sb("region_step", [P, NE]),
            "gap": sb("gap_all", [P, CH * NG]),
            "share": sb("share", [P, 2, CH * NG]),
            "table": sb("table", [1, TABLE], I32),
        }
        cst["started"] = ctx.enter_context(nc.semaphore("constants_ready"))
        with nc.semaphore("filled") as filled, nc.Block() as block:
            @block.gpsimd
            def _(pool):
                nc.gpsimd.memset(cst["zero1"][:], 0.0)
                nc.gpsimd.memset(cst["half"][:], -0.5)
                for n in ("ident", "le", "gt", "lt", "ones"):
                    i = nc.gpsimd.memset(cst[n][:], 0.0 if n == "ident" else 1.0)
                i.then_inc(filled, 1)
                pool.wait_ge(filled, 1)
                for n, op, mult, step in (("ident", ALU.not_equal, 1, -1), ("le", ALU.is_ge, -1, 1),
                                          ("gt", ALU.is_gt, 1, -1), ("lt", ALU.is_gt, -1, 1)):
                    m = cst[n][:]
                    i = nc.gpsimd.affine_select(out=m, in_=m, compare_op=op, fill=1.0 if n == "ident" else 0.0,
                                                base=0, pattern=[[step, P]], channel_multiplier=mult)
                i.then_inc(cst["started"], 1)
                pool.wait_ge(cst["started"], 1)
        mamba_phase(nc, io, dram, cst, routing)
        cst["ffn_w"] = sb("ffn_w", [P, FFN_W], F32R)
        expert_phase(nc, io, dram, cst, routing)
        ffn_phase(nc, io, dram, cst, routing, out)


def kernel(**inputs):
    import numpy as np
    import concourse.bacc as bacc
    from concourse.bass_utils import run_bass_kernel_spmd

    def arr(name):
        return np.asarray(inputs[name])

    def cols(a, k):
        return np.ascontiguousarray(np.moveaxis(a.reshape(k, P, *a.shape[1:]), 0, 1))

    w1 = arr("L0_attn_w1").transpose(0, 2, 1).reshape(NE, KD, P, FF).transpose(0, 2, 1, 3).reshape(NE, P, KD * FF)
    w2 = arr("L0_attn_w2").transpose(0, 2, 1).reshape(NE, KF, P, D).transpose(0, 2, 1, 3).reshape(NE, P, KF * D)
    ffn = [cols(arr("L0_ffn_w_gate"), KD), cols(arr("L0_ffn_w_up"), KD), cols(arr("L0_ffn_w_down"), KF)]
    arrays = {
        "x": arr("L0_attn_x").reshape(NG, CH, P, D).transpose(0, 2, 1, 3),
        "in_w": cols(arr("L0_attn_in_proj_w").T, KD),
        "out_w": cols(arr("L0_attn_out_proj_w").T, KI),
        "gate_w": cols(arr("L0_attn_gate_w").T, KD),
        "conv_w": cols(arr("L0_attn_conv_w"), KC),
        "conv_b": cols(arr("L0_attn_conv_b"), KC),
        "d_col": cols(np.repeat(arr("L0_attn_D"), HD), KI),
        "ssm_w": cols(arr("L0_attn_ssm_norm_w"), KI),
        "nm_w": cols(arr("L0_attn_norm_mamba_w"), KD),
        "moe_w": cols(arr("L0_attn_norm_moe_w"), KD),
        "dt_bias": arr("L0_attn_dt_bias"),
        "a_log": arr("L0_attn_A_log"),
        "w12": np.concatenate([w1, w2], axis=2),
        "ffn_w": np.ascontiguousarray(np.concatenate([a.reshape(P, -1) for a in ffn], axis=1)).view(np.int32),
        "s_gu": np.stack([cols(arr("L0_ffn_s_gate"), KF), cols(arr("L0_ffn_s_up"), KF)], axis=1),
        "s_down": arr("L0_ffn_s_down"),
    }
    arrays = {f"in_{n}": np.ascontiguousarray(a) for n, a in arrays.items()}
    nc = bacc.Bacc("TRN2", target_bir_lowering=False, num_devices=1)
    io = {n[3:]: nc.dram_tensor(n, a.shape, mybir.dt.from_np(a.dtype), kind="ExternalInput").ap()
          for n, a in arrays.items()}
    out = nc.dram_tensor("out", [NG, P, CH, D], F32, kind="ExternalOutput").ap()
    build(nc, io, out)
    r = run_bass_kernel_spmd(nc, [arrays], core_ids=[0])
    got = r.results[0]["out"]
    return np.ascontiguousarray(np.asarray(got).transpose(0, 2, 1, 3)).reshape(B, L, D)
```

```python
from contextlib import ExitStack

import concourse.bass as bass
from concourse import mybir

F32 = mybir.dt.float32
F32R = mybir.dt.float32r
I32 = mybir.dt.int32
U32 = mybir.dt.uint32
I8 = mybir.dt.int8
ALU = mybir.AluOpType
ACT = mybir.ActivationFunctionType
AX = mybir.AxisListType

P = 128
D = 256
KD = D // P
B, L = 4, 1024
T = B * L
DI = 512
KI = DI // P
NS = 64
NH = 8
HD = DI // NH
CONV = DI + 2 * NS
KC = CONV // P
TAPS = 4
PROJ = 2 * DI + 2 * NS + NH
COL_X, COL_BC, COL_DT = DI, 2 * DI, 2 * DI + 2 * NS
GT = 512
CH = GT // P
NG = T // GT
NE = 8
FF = 1024
KF = FF // P
ROWS = 256
RT = ROWS // P
REGION = T + ROWS
RMS_EPS = 1e-6
LN_EPS = 1e-5
A_LOG_MAX = 80.0
DECAY_MIN = -1e30
SMALL = 1.0 / 64

SOFT_LINKS = 11
ROUTE_LINKS = 14
SMALL_DMAS = 8 + 2 * CH
TILES = KC + KI
ITEMS, FIRST, PAD_ROW, TABLE = 0, NE + 1, 2 * NE + 2, 3 * NE + 2


def bcast(ap, dim, n):
    ap = ap.unsqueeze(dim)
    shape = list(ap.shape)
    shape[dim] = n
    return ap.to_broadcast(shape)


def flat(ap):
    return ap.rearrange("p a b -> p (a b)")


def wait(eng, sem, value):
    if not (isinstance(value, int) and value == 0):
        eng.wait_ge(sem, value)


FFN_W = 2 * KD * FF + KF * D
MAX_ITEMS = 2 * T // ROWS + NE
LA_T = 4
FUSED, POOL_PARTS, PAIRS = 4, 5, (NG - 4) // 2
MIX_NORM, Y_NORM, MIX_LATE = 4, 7, 3


class Pass:

    def __init__(self, eng, sem):
        self.eng, self.sem, self.times, self.total = eng, sem, 1, 0

    def __call__(self):
        self.eng.sem_inc(self.sem, 1)
        self.total += self.times

    def done(self):
        self.eng.wait_ge(self.sem, self.total)


class Link:

    def __init__(self, eng, sem, base):
        self.eng, self.sem, self.base, self.n = eng, sem, base, 0

    def __call__(self, instruction, passed=None):
        self.n += 1
        instruction.then_inc(self.sem, 1)
        self.eng.wait_ge(self.sem, self.base + self.n)
        if passed:
            passed()


def mamba_phase(nc, io, dram, cst, routing):
    with ExitStack() as ctx:
        def sb(name, shape, dt=F32):
            return ctx.enter_context(nc.sbuf_tensor(name, shape, dt))

        def sem(name):
            return ctx.enter_context(nc.semaphore(name))

        ident, le, gt, lt, ones = cst["ident"], cst["le"], cst["gt"], cst["lt"], cst["ones"]
        half, zero1 = cst["half"], cst["zero1"]
        w_hi = sb("w_hi", [P, KD, PROJ], F32R)
        w_lo = sb("w_lo", [P, KD, PROJ], F32R)
        w_out = sb("w_out", [P, KI, D])
        gate_w = sb("gate_w", [P, KD, NE])
        ssm_w = sb("ssm_w", [P, KI])
        nm_w = sb("nm_w", [P, KD])
        moe_w = cst["moe_w"]
        conv_w = sb("conv_w", [P, KC, TAPS])
        conv_b = sb("conv_b", [P, KC])
        d_col = sb("d_col", [P, KI])
        dt_bias = sb("dt_bias", [P, CH, NH])
        a_log = sb("a_log", [P, CH, NH])
        a_neg = sb("a_neg", [P, CH, NH])
        x_in = sb("x_in", [P, 2, CH, D])
        squares = sb("squares", [P, CH, D])
        tail_squares = sb("tail_squares", [P, D])
        stat = sb("stat", [P, 3, CH])
        x_norm = sb("x_norm", [P, CH, D])
        h_hi = sb("h_hi", [P, KD, GT], F32R)
        h_lo = sb("h_lo", [P, KD, GT], F32R)
        soft = sb("soft", [P, 8, CH * NH])
        dt = sb("dt", [P, 2, CH * NH])
        la = sb("la", [P, CH * NH])
        pex = sb("pex", [P, 2, 3, CH * NH])
        la_t = sb("la_t", [P, LA_T, NH, P])
        decay = sb("decay", [P, 2, CH, NH, P])
        raw = sb("raw", [P, 2, KC, TAPS - 1 + GT])
        conv = sb("conv", [P, 2, GT])
        xbc = sb("xbc", [P, 2, KC, GT])
        c_low = sb("c_low", [NS, 2, GT])
        z_act = sb("z_act", [P, 2, KI, GT])
        cb = sb("cb", [P, P])
        b_tok = sb("b_tok", [P, NS])
        x_dt = sb("x_dt", [P, NH, HD])
        x_end = sb("x_end", [P, NH, HD])
        state = sb("state", [NS, NH, HD])
        state_p = sb("state_p", [NS, NH, HD])
        y_in = sb("y_in", [P, NH, HD])
        y_tok = sb("y_tok", [P, NH, HD])
        y_d = sb("y_d", [P, KI, P])
        y_gated = sb("y_gated", [P, KI, P])
        y_sq = sb("y_sq", [P, KI, P])
        tail_stat = sb("tail_stat", [P, 8])
        h1 = sb("h1", [P, D])
        x_res = sb("x_res", [P, 2, CH, D])
        xm = sb("xm", [P, 2, CH, D])
        xm_t = sb("xm_t", [P, KD, P])
        logits = sb("logits", [P, CH, NE])
        top = sb("top", [P, CH, 8])
        top_i = sb("top_i", [P, CH, 8], U32)
        top_f = sb("top_f", [P, CH, 8])
        hot = sb("hot", [P, 3, CH, NE])
        run = sb("run", [P, CH + 1, NE])
        rank = sb("rank", [P, CH, NE])
        picked = sb("picked", [P, 2, CH, NE])
        row_f = sb("row_f", [P, CH, 2])
        row_u = sb("row_u", [P, 2, CH * 2], U32)
        iota_e = sb("iota_e", [P, NE])
        base_e = sb("base_e", [P, NE])
        items_i = sb("items_i", [P, NE], I32)
        rows_all, gap_all = routing["rows"], routing["gap"]

        bank = [ctx.enter_context(nc.psum_tensor(f"bank{i}", [P, 512], F32)) for i in range(8)]
        proj_ps = bank[0:2]
        dt_ps, cum_ps, rank_ps = bank[0][:, 0:32], bank[0][:, 0:96], bank[1][:, 0:64]
        out_ps, ss_ps = bank[2][:, 0:D], bank[2][:, D:D + 1]
        xmt_ps, logit_ps = bank[2][:, D:2 * D], bank[2][:, 0:NE]
        x_ps = bank[3]
        yt_ps, intra_ps, inter_ps = bank[4], bank[5], bank[6]
        cb_ps, bt_ps = bank[7][:, 0:P], bank[7][:, P:2 * P]

        s = {n: sem(n) for n in (
            "weights_in", "small_in", "masks", "w_split", "w_scaled", "a_exp", "a_ready", "iota_ready",
            "x_loaded", "ss_ready", "ms_ready", "rs_ready", "xn_ready", "ht_ps", "h_hi_ready",
            "h_lo_ready", "dt_done", "soft_in", "soft_exp", "soft_link", "la_ready", "cum_done",
            "pex_ready", "lat_ready", "seg_ps", "decay_ready", "tile_ps", "tile_out", "conv_link",
            "conv_ready", "xbc_ready", "c_moved", "halo_ready", "state_zero",
            "s1_done", "b_ready", "cb_ready", "xdt_ready", "m_ready", "xend_ready", "statep_ready",
            "inter_done", "intra_done", "state_done", "state_ready", "yin_ready", "ytok_ready",
            "yt_done", "yd_ready", "yg_ready", "ysq_ready", "out_done", "ms2_ready", "rs2_ready",
            "h1_ready", "xres_ready", "ss3_ready", "ms3_ready", "rs3_ready", "xm_ready", "xmt_done",
            "xmt_ready", "logit_done", "logit_ready", "route_link", "hot_ready", "rank_done",
            "rows_ready", "pool_passed", "dve_passed", "xres_stored", "xm_sent", "counts_link")}

        block = ctx.enter_context(nc.Block())


        @block.sync
        def _(sp):
            sp.dma_start(x_in[:, 0], io["x"][0]).then_inc(s["x_loaded"], 16)
            w_stage = decay[:].rearrange("p a b c d -> p (a b c d)")[:, 0:KD * PROJ]\
                .rearrange("p (k n) -> p k n", k=KD)
            sp.dma_start(w_stage, io["in_w"]).then_inc(s["weights_in"], 16)
            for dst, src in ((nm_w, "nm_w"), (conv_w, "conv_w"), (conv_b, "conv_b"), (d_col, "d_col"),
                             (ssm_w, "ssm_w"), (moe_w, "moe_w"), (gate_w, "gate_w")):
                sp.dma_start(dst[:], io[src]).then_inc(s["small_in"], 16)
            for dst, src in ((dt_bias, "dt_bias"), (a_log, "a_log")):
                for c in range(CH):
                    sp.dma_start(dst[:, c, :], io[src].partition_broadcast(P)).then_inc(s["small_in"], 16)
            sp.dma_start(w_out[:], io["out_w"]).then_inc(s["small_in"], 16)

            def project(g, j):
                sp.wait_ge(s["xbc_ready"], KC * g + 1)
                sp.dma_start(c_low[:, j], xbc[NS:2 * NS, j, KC - 1, :]).then_inc(s["c_moved"], 16)

            def scan(g, j, tail, more):
                if more:
                    wait(sp, s["xres_ready"], CH * g)
                    sp.dma_start(x_in[:, 1 - j], io["x"][g + 1]).then_inc(s["x_loaded"], 16)
                if tail:
                    store(g - 1, 1 - j)
                if more:
                    project(g + 1, 1 - j)

            def store(g, j):
                wait(sp, s["xres_stored"], 16 * g)
                sp.wait_ge(s["xres_ready"], CH * (g + 1))
                sp.dma_start(dram["x_res"][g], x_res[:, j]).then_inc(s["xres_stored"], 16)

            project(0, 0)
            scan(0, 0, False, True)
            with sp.Fori(0, (NG - 2) // 2) as b:
                scan(2 * b + 1, 1, True, True)
                scan(2 * b + 2, 0, True, True)
            scan(NG - 1, (NG - 1) % 2, True, False)
            store(NG - 1, (NG - 1) % 2)
            sp.wait_ge(s["xres_stored"], 16 * NG)
            sp.wait_ge(s["c_moved"], 16 * NG)

        @block.gpsimd
        def _(pool):
            passed = Pass(pool, s["pool_passed"])
            nc.gpsimd.iota(iota_e[:], pattern=[[1, NE]], base=0, channel_multiplier=0,
                           allow_small_or_imprecise_dtypes=True).then_inc(s["iota_ready"], 1)
            nc.gpsimd.iota(base_e[:], pattern=[[REGION, NE]], base=0, channel_multiplier=0,
                           allow_small_or_imprecise_dtypes=True).then_inc(s["iota_ready"], 1)

            def fill_norm(g, j):
                pool.wait_ge(s["ms_ready"], g + 1)
                nc.gpsimd.tensor_tensor(stat[:, 2, :], stat[:, 1, :], half[:], ALU.pow)\
                    .then_inc(s["rs_ready"], 1)

            def fill_seg(g, j, c):
                pool.wait_ge(s["la_ready"], g + 1)
                wait(pool, s["seg_ps"], seg_count(g, c))
                nc.gpsimd.tensor_tensor(la_t[:, c % LA_T], bcast(la[:, c * NH:(c + 1) * NH], 2, P),
                                        bcast(le[:], 1, NH), ALU.mult).then_inc(s["lat_ready"], 1)

            def seg_count(g, c):
                n = 2 * CH * g + 2 * (c + 1 - LA_T)
                return max(n, 0) if isinstance(n, int) else n

            def tail_norm(q):
                pool.wait_ge(s["ms2_ready"], q + 1)
                nc.gpsimd.tensor_tensor(tail_stat[:, 1:2], tail_stat[:, 0:1], half[:, 0:1], ALU.pow)\
                    .then_inc(s["rs2_ready"], 1)

            def tail_norm3(q):
                pool.wait_ge(s["ms3_ready"], q + 1)
                nc.gpsimd.tensor_tensor(tail_stat[:, 4:5], tail_stat[:, 3:4], half[:, 0:1], ALU.pow)\
                    .then_inc(s["rs3_ready"], 1)

            def send(g, j, chunks):
                if chunks[0] == 0:
                    pool.wait_ge(s["rows_ready"], g + 1)
                    wait(pool, s["xm_sent"], 16 * 2 * CH * g)
                    passed()
                for c in chunks:
                    for k in range(2):
                        n = 2 * c + k
                        nc.gpsimd.indirect_dma_start(
                            out=dram["sent"], out_offset=bass.IndirectOffsetOnAxis(ap=row_u[:, j, n:n + 1], axis=0),
                            in_=xm[:, j, c, :], in_offset=None).then_inc(s["xm_sent"], 16)

            def chunk(g, j, c, t, q):
                if c == 0 and j == 0:
                    wait(pool, s["inter_done"], q)
                    wait(pool, s["state_ready"], q)
                    passed()
                    nc.gpsimd.memset(state[:], 0.0).then_inc(s["state_zero"], 1)
                    pool.wait_ge(s["state_zero"], zeroed(g))
                if t:
                    tail_norm(q - 1)
                pool.wait_ge(s["xdt_ready"], q + 1)
                pool.wait_ge(s["pex_ready"], g + 1)
                nc.gpsimd.tensor_tensor(x_end[:], x_dt[:], bcast(pex[:, j, 1, c * NH:(c + 1) * NH], 2, HD),
                                        ALU.mult).then_inc(s["xend_ready"], 1)
                wait(pool, s["state_ready"], q)
                nc.gpsimd.tensor_tensor(state_p[:], state[:], bcast(pex[0:NS, j, 2, c * NH:(c + 1) * NH], 2, HD),
                                        ALU.mult).then_inc(s["statep_ready"], 1)

            def zeroed(g):
                return g // 2 + 1 if isinstance(g, int) else zero_index[0]

            zero_index = [None]

            def scan(g, j, tail, more):
                f = lambda fn, *a: fn(g + 1, 1 - j, *a) if more else None
                for c in range(CH):
                    q = CH * g + c
                    t = tail or c > 0
                    chunk(g, j, c, t, q)
                    if t:
                        tail_norm3(q - 1)
                    if c == 0:
                        f(fill_norm)
                    if c == 1:
                        for n in range(CH):
                            f(fill_seg, n)
                    if c == 2:
                        if tail:
                            send(g - 1, 1 - j, (0, 1))
                    if c == 3 and tail:
                        send(g - 1, 1 - j, (2, 3))

            fill_norm(0, 0)
            for i in range(CH):
                fill_seg(0, 0, i)
            scan(0, 0, False, True)
            with pool.Fori(0, (NG - 2) // 2) as b:
                zero_index[0] = b + 2
                passed.times = (NG - 2) // 2
                scan(2 * b + 1, 1, True, True)
                scan(2 * b + 2, 0, True, True)
                passed.times = 1
            scan(NG - 1, (NG - 1) % 2, True, False)
            tail_norm(CH * NG - 1)
            tail_norm3(CH * NG - 1)
            send(NG - 1, (NG - 1) % 2, (0, 1, 2, 3))
            pool.wait_ge(s["xm_sent"], 16 * 2 * CH * NG)
            passed.done()

        @block.scalar
        def _(act):
            act.wait_ge(s["a_exp"], 1)
            nc.scalar.activation(a_neg[:], a_neg[:], ACT.Exp).then_inc(s["a_exp"], 1)

            def norm_sums(g, j):
                act.wait_ge(s["x_loaded"], 16 * (g + 1))
                wait(act, s["ms_ready"], g)
                wait(act, s["ss_ready"], CH * g)
                for c in range(CH):
                    nc.scalar.activation(squares[:, c], x_in[:, j, c, :], ACT.Square,
                                         accum_out=stat[:, 0, c:c + 1]).then_inc(s["ss_ready"], 1)

            def h_parts(g, j):
                for k in range(KD):
                    act.wait_ge(s["ht_ps"], KD * g + k + 1)
                    nc.scalar.activation(h_hi[:, k], proj_ps[k][:], ACT.Copy, scale=nm_w[:, k:k + 1])\
                        .then_inc(s["h_hi_ready"], 1)

            def softplus(g, j):
                act.wait_ge(s["soft_in"], g + 1)
                nc.scalar.activation(soft[:, 2], soft[:, 1], ACT.Exp).then_inc(s["soft_exp"], 1)
                act.wait_ge(s["soft_exp"], 2 * g + 1)
                nc.scalar.activation(soft[:, 3], soft[:, 2], ACT.Ln, bias=1.0).then_inc(s["soft_exp"], 1)

            def sums_exp(g, j):
                act.wait_ge(s["cum_done"], g + 1)
                nc.scalar.activation(flat(pex[:, j]), cum_ps, ACT.Exp).then_inc(s["pex_ready"], 1)

            def seg_exp(g, j, c):
                for h in range(2):
                    n = 2 * c + h
                    act.wait_ge(s["seg_ps"], 2 * CH * g + n + 1)
                    nc.scalar.activation(flat(decay[:, j, c])[:, h * GT:(h + 1) * GT], proj_ps[n % 2][:], ACT.Exp)\
                        .then_inc(s["decay_ready"], 1)

            def tile_out(g, j, i):
                act.wait_ge(s["tile_ps"], TILES * g + i + 1)
                if i < KC:
                    k = (i + KC - 1) % KC
                    wait(act, s["conv_ready"], KC * g)
                    nc.scalar.activation(raw[:, j, k, TAPS - 1:], proj_ps[i % 2][:], ACT.Identity)\
                        .then_inc(s["tile_out"], 1)
                else:
                    nc.scalar.activation(z_act[:, j, i - KC, :], proj_ps[i % 2][:], ACT.Silu)\
                        .then_inc(s["tile_out"], 1)

            def conv_out(g, j, n):
                k = (n + KC - 1) % KC
                act.wait_ge(s["conv_ready"], KC * g + n + 1)
                nc.scalar.activation(xbc[:, j, k, :], conv[:, n % 2, :], ACT.Silu)\
                    .then_inc(s["xbc_ready"], 1)

            def tail_square(q):
                act.wait_ge(s["h1_ready"], q + 1)
                wait(act, s["ms3_ready"], q)
                wait(act, s["ss3_ready"], q)
                nc.scalar.activation(tail_squares[:], h1[:], ACT.Square, accum_out=tail_stat[:, 2:3])\
                    .then_inc(s["ss3_ready"], 1)

            def tail_xmt(q):
                act.wait_ge(s["xmt_done"], q + 1)
                wait(act, s["logit_done"], q)
                for k in range(KD):
                    nc.scalar.activation(xm_t[:, k], xmt_ps[:, k * P:(k + 1) * P], ACT.Copy,
                                         scale=moe_w[:, k:k + 1]).then_inc(s["xmt_ready"], 1)

            def scan(g, j, tail, more):
                f = lambda fn, *a: fn(g + 1, 1 - j, *a) if more else None
                for c in range(CH):
                    q = CH * g + c
                    t = tail or c > 0
                    if t:
                        tail_square(q - 1)
                    if c == 2:
                        f(seg_exp, 1)
                        f(seg_exp, 2)
                    if c == 3:
                        f(tile_out, 3)
                        f(conv_out, 1)
                    if c == 1:
                        f(softplus)
                    if t:
                        tail_xmt(q - 1)
                    if c == 0:
                        f(norm_sums)
                    if c == 2:
                        f(seg_exp, 3)
                        f(tile_out, 0)
                    if c == 3:
                        f(tile_out, 4)
                        f(tile_out, 5)
                        f(conv_out, 2)
                    act.wait_ge(s["yg_ready"], q + 1)
                    nc.scalar.activation(y_sq[:], y_gated[:], ACT.Square).then_inc(s["ysq_ready"], 1)
                    if c == 0:
                        f(h_parts)
                    if c == 1:
                        f(sums_exp)
                        f(seg_exp, 0)
                    if c == 2:
                        f(tile_out, 1)
                        f(tile_out, 2)
                        f(conv_out, 0)
                    if c == 3:
                        f(tile_out, 6)
                        f(conv_out, 3)
                        f(conv_out, 4)
                        f(tile_out, 7)
                        f(tile_out, 8)

            act.wait_ge(s["small_in"], 16 * SMALL_DMAS)
            norm_sums(0, 0)
            h_parts(0, 0)
            softplus(0, 0)
            sums_exp(0, 0)
            for i in range(CH):
                seg_exp(0, 0, i)
            for i in range(TILES):
                tile_out(0, 0, i)
                if 1 <= i <= KC:
                    conv_out(0, 0, i - 1)
            scan(0, 0, False, True)
            with act.Fori(0, (NG - 2) // 2) as b:
                scan(2 * b + 1, 1, True, True)
                scan(2 * b + 2, 0, True, True)
            scan(NG - 1, (NG - 1) % 2, True, False)
            tail_square(CH * NG - 1)
            tail_xmt(CH * NG - 1)

        @block.tensor
        def _(pe):
            mm = nc.tensor.matmul

            def split_mm(out, a_hi, a_lo, b_hi, b_lo, first, last):
                mm(out, a_hi, b_hi, start=first, stop=False)
                mm(out, a_hi, b_lo, start=False, stop=False)
                return mm(out, a_lo, b_hi, start=False, stop=last)

            def transposes(g, j):
                for k in range(KD):
                    wait(pe, s["tile_out"], TILES * g)
                    for c in range(CH):
                        if k == 0:
                            pe.wait_ge(s["xn_ready"], CH * g + c + 1)
                        i = nc.tensor.transpose(proj_ps[k][:, c * P:(c + 1) * P],
                                                x_norm[:, c, k * P:(k + 1) * P], ident[:])
                    i.then_inc(s["ht_ps"], 1)

            def dt_proj(g, j):
                pe.wait_ge(s["h_lo_ready"], KD * (g + 1))
                if isinstance(g, int) and g == 0:
                    pe.wait_ge(s["w_split"], 4)
                for c in range(CH):
                    for k in range(KD):
                        t = slice(c * P, (c + 1) * P)
                        i = split_mm(dt_ps[:, c * NH:(c + 1) * NH], h_hi[:, k, t], h_lo[:, k, t],
                                     w_hi[:, k, COL_DT:], w_lo[:, k, COL_DT:], k == 0, k == KD - 1)
                i.then_inc(s["dt_done"], 1)

            def sums(g, j):
                pe.wait_ge(s["la_ready"], g + 1)
                for n, m in enumerate((le, gt, ones)):
                    i = mm(cum_ps[:, 32 * n:32 * n + 32], m[:], la[:], start=True, stop=True)
                i.then_inc(s["cum_done"], 1)

            def seg(g, j, c):
                pe.wait_ge(s["lat_ready"], CH * g + c + 1)
                for h in range(2):
                    n = 2 * c + h
                    if n == 0:
                        pe.wait_ge(s["pex_ready"], g + 1)
                    elif n == 1:
                        pe.wait_ge(s["h_lo_ready"], KD * (g + 1))
                        wait(pe, s["rows_ready"], g - 1 if not isinstance(g, int) else max(g - 1, 0))
                    else:
                        pe.wait_ge(s["decay_ready"], 2 * CH * g + n - 1)
                    mm(proj_ps[n % 2][:], gt[:], flat(la_t[:, c % LA_T])[:, h * GT:(h + 1) * GT], start=True, stop=True)\
                        .then_inc(s["seg_ps"], 1)

            def tile(g, j, i):
                if i < 2:
                    pe.wait_ge(s["decay_ready"], 2 * CH * (g + 1) - 1 + i)
                else:
                    pe.wait_ge(s["tile_out"], TILES * g + i - 1)
                col = COL_BC if i == 0 else COL_X + (i - 1) * P if i < KC else (i - KC) * P
                for k in range(KD):
                    r = split_mm(proj_ps[i % 2][:], w_hi[:, k, col:col + P], w_lo[:, k, col:col + P],
                                 h_hi[:, k, :], h_lo[:, k, :], k == 0, k == KD - 1)
                r.then_inc(s["tile_ps"], 1)

            def s1(g, j, c, q):
                if c == 0:
                    pe.wait_ge(s["xbc_ready"], KC * (g + 1))
                    pe.wait_ge(s["c_moved"], 16 * (g + 1))
                t = slice(c * P, (c + 1) * P)
                wait(pe, s["state_ready"], q)
                wait(pe, s["b_ready"], q)
                for k in range(KI):
                    nc.tensor.transpose(x_ps[:, k * P:(k + 1) * P], xbc[:, j, k, t], ident[:])
                nc.tensor.transpose(bt_ps, xbc[:, j, KC - 1, t], ident[:])
                wait(pe, s["cb_ready"], q)
                mm(cb_ps, xbc[0:NS, j, KC - 1, t], c_low[:, j, t], start=True, stop=True)\
                    .then_inc(s["s1_done"], 1)
                if c == 0 and j == 0:
                    pe.wait_ge(s["state_zero"], g // 2 + 1 if isinstance(g, int) else zero_index[0])
                wait(pe, s["yin_ready"], q)
                mm(inter_ps[:], c_low[:, j, t], flat(state[:]), start=True, stop=True)\
                    .then_inc(s["inter_done"], 1)

            def s3(g, j, c, q):
                pe.wait_ge(s["m_ready"], q + 1)
                pe.wait_ge(s["xdt_ready"], q + 1)
                wait(pe, s["ytok_ready"], q)
                for h in range(NH):
                    i = mm(intra_ps[:, h * HD:(h + 1) * HD], decay[:, j, c, h, :], x_dt[:, h, :],
                           start=True, stop=True)
                i.then_inc(s["intra_done"], 1)
                pe.wait_ge(s["xend_ready"], q + 1)
                pe.wait_ge(s["b_ready"], q + 1)
                mm(x_ps[0:NS, :], b_tok[:], flat(x_end[:]), start=True, stop=True).then_inc(s["state_done"], 1)

            def s5(q):
                pe.wait_ge(s["ytok_ready"], q + 1)
                wait(pe, s["yd_ready"], KI * q)
                for k in range(KI):
                    i = nc.tensor.transpose(yt_ps[:, k * P:(k + 1) * P], flat(y_tok[:])[:, k * P:(k + 1) * P], ident[:])
                i.then_inc(s["yt_done"], 1)

            def s6(q):
                pe.wait_ge(s["yg_ready"], q + 1)
                pe.wait_ge(s["ysq_ready"], q + 1)
                wait(pe, s["logit_ready"], q)
                for k in range(KI):
                    mm(out_ps, y_gated[:, k, :], w_out[:, k, :], start=k == 0, stop=k == KI - 1)
                for k in range(KI):
                    i = mm(ss_ps, y_sq[:, k, :], ones[:, 0:1], start=k == 0, stop=k == KI - 1)
                i.then_inc(s["out_done"], 1)

            def tail_t(q):
                pe.wait_ge(s["xm_ready"], q + 1)
                wait(pe, s["xmt_ready"], KD * q)
                for k in range(KD):
                    c = tail_chunk[0]
                    i = nc.tensor.transpose(xmt_ps[:, k * P:(k + 1) * P],
                                            xm[:, tail_parity[0], c, k * P:(k + 1) * P], ident[:])
                i.then_inc(s["xmt_done"], 1)

            def tail_logits(q):
                pe.wait_ge(s["xmt_ready"], KD * (q + 1))
                wait(pe, s["logit_ready"], q)
                for k in range(KD):
                    i = mm(logit_ps, xm_t[:, k], gate_w[:, k], start=k == 0, stop=k == KD - 1)
                i.then_inc(s["logit_done"], 1)

            def ranks(g, more):
                pe.wait_ge(s["hot_ready"], g + 1)
                if not more:
                    pe.wait_ge(s["tile_out"], TILES * NG)
                    pe.wait_ge(s["rows_ready"], g)
                mm(rank_ps[:, 0:32], lt[:], flat(hot[:, 2]), start=True, stop=True)
                mm(rank_ps[:, 32:64], ones[:], flat(hot[:, 2]), start=True, stop=True).then_inc(s["rank_done"], 1)

            tail_chunk, tail_parity, zero_index = [0], [0], [None]

            def scan(g, j, tail, more):
                f = lambda fn, *a: fn(g + 1, 1 - j, *a) if more else None
                for c in range(CH):
                    q = CH * g + c
                    t = tail or c > 0
                    tail_chunk[0], tail_parity[0] = (c - 1) % CH, j if c else 1 - j
                    s1(g, j, c, q)
                    if c == 1:
                        f(dt_proj)
                        if tail:
                            ranks(g - 1, more)
                    if c == 2:
                        f(seg, 1)
                        f(seg, 2)
                    if c == 3:
                        f(tile, 3)
                    s3(g, j, c, q)
                    if t:
                        tail_t(q - 1)
                    if c == 2:
                        f(seg, 3)
                        f(tile, 0)
                    if c == 3:
                        f(tile, 4)
                        f(tile, 5)
                    s5(q)
                    if t:
                        tail_logits(q - 1)
                    if c == 1:
                        f(sums)
                    if c == 2:
                        f(tile, 1)
                    if c == 3:
                        f(tile, 6)
                    s6(q)
                    if c == 0:
                        f(transposes)
                    if c == 1:
                        f(seg, 0)
                    if c == 2:
                        f(tile, 2)
                    if c == 3:
                        f(tile, 7)
                        f(tile, 8)

            transposes(0, 0)
            dt_proj(0, 0)
            sums(0, 0)
            for i in range(CH):
                seg(0, 0, i)
            for i in range(TILES):
                tile(0, 0, i)
            pe.wait_ge(s["w_scaled"], 1)
            scan(0, 0, False, True)
            with pe.Fori(0, (NG - 2) // 2) as b:
                zero_index[0] = b + 2
                scan(2 * b + 1, 1, True, True)
                scan(2 * b + 2, 0, True, True)
            scan(NG - 1, (NG - 1) % 2, True, False)
            tail_chunk[0], tail_parity[0] = CH - 1, (NG - 1) % 2
            tail_t(CH * NG - 1)
            tail_logits(CH * NG - 1)
            ranks(NG - 1, False)

        @block.vector
        def _(dve):
            passed = Pass(dve, s["dve_passed"])
            tt, stt, ts = nc.vector.tensor_tensor, nc.vector.scalar_tensor_tensor, nc.vector.tensor_scalar
            dve.wait_ge(s["small_in"], 16 * SMALL_DMAS)
            ts(a_neg[:], a_log[:], A_LOG_MAX, None, ALU.min).then_inc(s["a_exp"], 1)
            nc.vector.memset(raw[:, 0, :, 0:TAPS - 1], 0.0).then_inc(s["halo_ready"], 1)
            dve.wait_ge(s["iota_ready"], 2)
            nc.vector.tensor_copy(run[:, 0, :], base_e[:]).then_inc(s["counts_link"], 1)
            for k in range(KI):
                i = ts(w_out[:, k, :], w_out[:, k, :], ssm_w[:, k:k + 1], None, ALU.mult)
            i.then_inc(s["w_scaled"], 1)
            dve.wait_ge(s["a_exp"], 2)
            ts(a_neg[:], a_neg[:], -1.0, None, ALU.mult).then_inc(s["a_ready"], 1)
            w_stage = decay[:].rearrange("p a b c d -> p (a b c d)")[:, 0:KD * PROJ]\
                .rearrange("p (k n) -> p k n", k=KD)
            dve.wait_ge(s["weights_in"], 16)
            for k in range(KD):
                nc.vector.tensor_copy(w_hi[:, k], w_stage[:, k]).then_inc(s["w_split"], 1)
            for k in range(KD):
                dve.wait_ge(s["w_split"], k + 1)
                tt(w_lo[:, k], w_stage[:, k], w_hi[:, k].bitcast(F32), ALU.subtract)\
                    .then_inc(s["w_split"], 1)

            def norm(g, j):
                dve.wait_ge(s["ss_ready"], CH * (g + 1))
                ts(stat[:, 1, :], stat[:, 0, :], 1.0 / D, RMS_EPS, ALU.mult, ALU.add)\
                    .then_inc(s["ms_ready"], 1)
                dve.wait_ge(s["rs_ready"], g + 1)
                wait(dve, s["ht_ps"], KD * g)
                for c in range(CH):
                    ts(x_norm[:, c, :], x_in[:, j, c, :], stat[:, 2, c:c + 1], None, ALU.mult)\
                        .then_inc(s["xn_ready"], 1)

            def h_parts(g, j):
                for k in range(KD):
                    dve.wait_ge(s["h_hi_ready"], KD * g + k + 1)
                    stt(h_lo[:, k], proj_ps[k][:], nm_w[:, k:k + 1], h_hi[:, k].bitcast(F32),
                        ALU.mult, ALU.subtract).then_inc(s["h_lo_ready"], 1)

            def softplus_in(g, j):
                link = Link(dve, s["soft_link"], SOFT_LINKS * g)
                v = soft[:, 0]
                dve.wait_ge(s["dt_done"], g + 1)
                link(tt(v, dt_ps, flat(dt_bias[:]), ALU.add))
                stt(soft[:, 1], v, -1.0, v, ALU.mult, ALU.min).then_inc(s["soft_in"], 1)
                return link

            def softplus_out(g, j, link):
                v, u, ln = soft[:, 0], soft[:, 2], soft[:, 3]
                p, m, d = soft[:, 4], soft[:, 5], soft[:, 6]
                dve.wait_ge(s["soft_exp"], 2 * (g + 1))
                link(ts(p, u, -0.25, 1.0 / 3, ALU.mult, ALU.add))
                link(tt(d, p, u, ALU.mult))
                link(stt(p, d, -0.5, u, ALU.add, ALU.mult))
                link(stt(d, p, 1.0, u, ALU.add, ALU.mult))
                link(tt(p, d, ln, ALU.subtract))
                link(ts(m, u, SMALL, None, ALU.is_lt))
                link(tt(d, p, m, ALU.mult))
                link(tt(p, d, ln, ALU.add))
                link(stt(dt[:, j], v, 0.0, p, ALU.max, ALU.add))
                link(tt(m, dt[:, j], flat(a_neg[:]), ALU.mult))
                if not (isinstance(g, int) and g == 0):
                    dve.wait_ge(s["pex_ready"], g)
                    dve.wait_ge(s["seg_ps"], 2 * CH * g)
                ts(la[:], m, DECAY_MIN, None, ALU.max).then_inc(s["la_ready"], 1)
                assert link.n == SOFT_LINKS

            def convolve(g, j, i):
                k = (i + KC - 1) % KC
                n = KC * g + i
                dve.wait_ge(s["tile_out"], TILES * g + i + 1)
                if i == 0 and j == 1:
                    nc.vector.tensor_copy(raw[:, 1, :, 0:TAPS - 1], raw[:, 0, :, GT:])\
                        .then_inc(s["halo_ready"], 1)
                    dve.wait_ge(s["halo_ready"], halo(g))
                wait(dve, s["xbc_ready"], n - 1 if i > 0 or not isinstance(g, int) else max(n - 1, 0))
                link = Link(dve, s["conv_link"], (TAPS - 1) * n)
                acc = conv[:, i % 2, :]
                link(ts(acc, raw[:, j, k, TAPS - 1:], conv_w[:, k, TAPS - 1:], conv_b[:, k:k + 1],
                        ALU.mult, ALU.add))
                for m in range(TAPS - 1):
                    r = stt(acc, raw[:, j, k, m:m + GT], conv_w[:, k, m:m + 1], acc, ALU.mult, ALU.add)
                    if m < TAPS - 2:
                        link(r)
                r.then_inc(s["conv_ready"], 1)

            def halo(g):
                return (g + 1) // 2 + 1 if isinstance(g, int) else halo_index[0]

            halo_index = [None]

            def front(g, j, c, q):
                dve.wait_ge(s["s1_done"], q + 1)
                tt(cb[:], cb_ps, le[:], ALU.mult).then_inc(s["cb_ready"], 1)
                nc.vector.tensor_copy(b_tok[:], bt_ps[:, 0:NS]).then_inc(s["b_ready"], 1)
                tt(x_dt[:], x_ps[:].rearrange("p (h d) -> p h d", h=NH),
                   bcast(dt[:, j, c * NH:(c + 1) * NH], 2, HD), ALU.mult).then_inc(s["xdt_ready"], 1)

            def weigh(g, j, c, q):
                dve.wait_ge(s["decay_ready"], 2 * CH * g + 2 * c + 2)
                dve.wait_ge(s["cb_ready"], q + 1)
                tt(decay[:, j, c], decay[:, j, c], bcast(cb[:], 1, NH), ALU.mult).then_inc(s["m_ready"], 1)

            def earlier(g):
                return max(g - 1, 0) if isinstance(g, int) else g - 1

            def tail_a(q):
                dve.wait_ge(s["out_done"], q + 1)
                ts(tail_stat[:, 0:1], ss_ps, 1.0 / DI, RMS_EPS, ALU.mult, ALU.add)\
                    .then_inc(s["ms2_ready"], 1)

            def tail_b(g, j, c, q):
                dve.wait_ge(s["rs2_ready"], q + 1)
                wait(dve, s["ss3_ready"], q)
                stt(h1[:], out_ps, tail_stat[:, 1:2], x_in[:, j, c, :], ALU.mult, ALU.add)\
                    .then_inc(s["h1_ready"], 1)
                dve.wait_ge(s["h1_ready"], q + 1)
                if c == 0:
                    wait(dve, s["xres_stored"], 16 * earlier(g))
                tt(x_res[:, j, c, :], h1[:], x_in[:, j, c, :], ALU.add).then_inc(s["xres_ready"], 1)

            def tail_c(g, j, c, q):
                dve.wait_ge(s["ss3_ready"], q + 1)
                ts(tail_stat[:, 3:4], tail_stat[:, 2:3], 1.0 / D, RMS_EPS, ALU.mult, ALU.add)\
                    .then_inc(s["ms3_ready"], 1)
                dve.wait_ge(s["rs3_ready"], q + 1)
                if c == 0:
                    wait(dve, s["xm_sent"], 16 * 2 * CH * earlier(g))
                ts(xm[:, j, c, :], h1[:], tail_stat[:, 4:5], None, ALU.mult).then_inc(s["xm_ready"], 1)

            def middle(g, j, c, q):
                dve.wait_ge(s["inter_done"], q + 1)
                wait(dve, s["ytok_ready"], q)
                tt(y_in[:], inter_ps[:].rearrange("p (h d) -> p h d", h=NH),
                   bcast(pex[:, j, 0, c * NH:(c + 1) * NH], 2, HD), ALU.mult).then_inc(s["yin_ready"], 1)
                dve.wait_ge(s["intra_done"], q + 1)
                dve.wait_ge(s["yin_ready"], q + 1)
                wait(dve, s["yt_done"], q)
                tt(y_tok[:], y_in[:], intra_ps[:].rearrange("p (h d) -> p h d", h=NH), ALU.add)\
                    .then_inc(s["ytok_ready"], 1)
                dve.wait_ge(s["statep_ready"], q + 1)
                dve.wait_ge(s["state_done"], q + 1)
                tt(state[:], state_p[:], x_ps[0:NS, :].rearrange("p (h d) -> p h d", h=NH), ALU.add)\
                    .then_inc(s["state_ready"], 1)

            def gate(g, j, c, q):
                t = slice(c * P, (c + 1) * P)
                dve.wait_ge(s["yt_done"], q + 1)
                wait(dve, s["yg_ready"], q)
                for k in range(KI):
                    stt(y_d[:, k, :], xbc[:, j, k, t], d_col[:, k:k + 1], yt_ps[:, k * P:(k + 1) * P],
                        ALU.mult, ALU.add).then_inc(s["yd_ready"], 1)
                dve.wait_ge(s["yd_ready"], KI * (q + 1))
                wait(dve, s["out_done"], q)
                if c == 0:
                    dve.wait_ge(s["tile_out"], TILES * (g + 1))
                tt(y_gated[:], y_d[:], z_act[:, j, :, t], ALU.mult).then_inc(s["yg_ready"], 1)

            def tail_d(g, c, q):
                dve.wait_ge(s["logit_done"], q + 1)
                nc.vector.tensor_copy(logits[:, c, :], logit_ps).then_inc(s["logit_ready"], 1)

            def route_a(g):
                link = Link(dve, s["route_link"], ROUTE_LINKS * g)
                dve.wait_ge(s["logit_ready"], CH * (g + 1))
                passed()
                for c in range(CH):
                    r = nc.vector.max(top[:, c, :], logits[:, c, :])
                link(r, passed)
                for c in range(CH):
                    r = nc.vector.max_index(top_i[:, c, :], top[:, c, :], logits[:, c, :])
                link(r)
                link(nc.vector.tensor_copy(top_f[:], top_i[:]))
                for k in range(2):
                    r = tt(hot[:, k], bcast(iota_e[:], 1, CH), top_f[:, :, k:k + 1].to_broadcast([P, CH, NE]),
                           ALU.is_equal)
                link(r)
                tt(hot[:, 2], hot[:, 0], hot[:, 1], ALU.add).then_inc(s["hot_ready"], 1)
                link(tt(gap_all[:, bass.ds(CH * g, CH)], top[:, :, 1], top[:, :, 0], ALU.subtract))
                return link

            def route_b(g, j, link):
                dve.wait_ge(s["rank_done"], g + 1)
                for c in range(CH):
                    link(tt(run[:, c + 1, :], run[:, c, :], rank_ps[:, 32 + c * NE:32 + (c + 1) * NE], ALU.add))
                link(tt(rank[:], run[:, 0:CH, :], rank_ps[:, 0:32].rearrange("p (c e) -> p c e", c=CH), ALU.add))
                for k in range(2):
                    r = tt(picked[:, k], rank[:], hot[:, k], ALU.mult)
                link(r)
                for k in range(2):
                    r = nc.vector.tensor_reduce(row_f[:, :, k], picked[:, k], AX.X, ALU.add)
                link(r)
                nc.vector.tensor_copy(row_u[:, j, :], flat(row_f[:]))\
                    .then_inc(s["rows_ready"], 1)
                link(nc.vector.tensor_copy(rows_all[:, bass.ds(2 * CH * g, 2 * CH)],
                                           flat(row_f[:])))
                link(nc.vector.tensor_copy(run[:, 0, :], run[:, CH, :]))
                assert link.n == ROUTE_LINKS, link.n

            def scan(g, j, tail, more):
                f = lambda fn, *a: fn(g + 1, 1 - j, *a) if more else None
                for c in range(CH):
                    q = CH * g + c
                    t = tail or c > 0
                    of = (g, j, c - 1, q - 1) if c else (g - 1, 1 - j, CH - 1, q - 1)
                    if t:
                        tail_a(q - 1)
                    front(g, j, c, q)
                    if t:
                        tail_b(*of)
                    weigh(g, j, c, q)
                    if t:
                        tail_c(*of)
                    if c == 1:
                        soft_link = f(softplus_in)
                    if c == 3:
                        f(convolve, 2)
                    middle(g, j, c, q)
                    if c == 1:
                        f(softplus_out, soft_link)
                    if c == 3:
                        f(convolve, 3)
                    gate(g, j, c, q)
                    if c == 1 and tail:
                        route_b(g - 1, 1 - j, links[0])
                    if t:
                        tail_d(of[0], of[2], q - 1)
                    if c == 0:
                        f(norm)
                        if tail:
                            links[0] = route_a(g - 1)
                        f(h_parts)
                    if c == 2:
                        f(convolve, 0)
                        f(convolve, 1)
                    if c == 3:
                        f(convolve, 4)

            links = [None]
            norm(0, 0)
            h_parts(0, 0)
            dve.wait_ge(s["a_ready"], 1)
            softplus_out(0, 0, softplus_in(0, 0))
            for i in range(KC):
                convolve(0, 0, i)
            scan(0, 0, False, True)
            with dve.Fori(0, (NG - 2) // 2) as b:
                halo_index[0] = b + 3
                passed.times = (NG - 2) // 2
                scan(2 * b + 1, 1, True, True)
                scan(2 * b + 2, 0, True, True)
                passed.times = 1
            scan(NG - 1, (NG - 1) % 2, True, False)
            q = CH * NG - 1
            of = (NG - 1, (NG - 1) % 2, CH - 1, q)
            tail_a(q)
            tail_b(*of)
            tail_c(*of)
            tail_d(of[0], of[2], q)
            link = route_a(NG - 1)
            route_b(NG - 1, (NG - 1) % 2, link)
            table = routing["table"]
            link = Link(dve, s["counts_link"], 1)
            row = slice(0, 1)
            end, n_rows, n_items, before = run[:, 0, :], run[:, 1, :], run[:, 2, :], run[:, 3, :]
            link(nc.vector.memset(table[:], 0))
            link(nc.vector.tensor_copy(table[:, PAD_ROW:PAD_ROW + NE], end[row]))
            link(tt(n_rows, end, base_e[:], ALU.subtract))
            link(ts(n_rows, n_rows, float(ROWS - 1), None, ALU.add))
            link(nc.vector.tensor_copy(items_i[:], n_rows))
            link(ts(items_i[:], items_i[:], ROWS.bit_length() - 1, None, ALU.arith_shift_right))
            link(nc.vector.tensor_copy(table[:, ITEMS:ITEMS + NE], items_i[row, :]))
            link(nc.vector.tensor_copy(n_items, items_i[:]))
            link(ts(routing["step"][:], n_items, float(ROWS), float(-REGION), ALU.mult, ALU.add))
            for e in range(NE):
                link(tt(before[:, e:e + 1], n_items[:, e:e + 1], before[:, e - 1:e] if e else zero1[:],
                        ALU.add))
            link(nc.vector.tensor_copy(table[:, FIRST + 1:FIRST + 1 + NE], before[row, :]))
            passed.done()


def expert_phase(nc, io, dram, cst, routing):
    with ExitStack() as ctx:
        def sb(name, shape, dt=F32):
            return ctx.enter_context(nc.sbuf_tensor("e_" + name, shape, dt))

        def sem(name):
            return ctx.enter_context(nc.semaphore("e_" + name))

        ident, moe_w, table = cst["ident"], cst["moe_w"], routing["table"]
        W1, W2 = KD * FF, KF * D
        stage = sb("stage", [P, W1 + W2])
        w_hi = sb("w_hi", [P, 2, W1 + W2], F32R)
        w_lo = sb("w_lo", [P, 2, W1 + W2], F32R)
        zeros = sb("zeros", [P, RT, D])
        x_rows = sb("x_rows", [P, RT, D])
        x_hi = sb("x_hi", [P, KD, ROWS], F32R)
        x_lo = sb("x_lo", [P, KD, ROWS], F32R)
        h_act = sb("h_act", [P, 2, 2 * ROWS])
        h_hi = sb("h_hi", [P, KF, ROWS], F32R)
        h_lo = sb("h_lo", [P, KF, ROWS], F32R)
        y_rows = sb("y_rows", [P, RT, D])
        w8 = sb("w8", [P, FFN_W], I8)
        moved = sb("moved", [P, 2 * CH * NG])
        shift = sb("shift", [P, 2 * CH * NG])
        share, gap_all = routing["share"], routing["gap"]
        pairs = KF // 2
        bank = [ctx.enter_context(nc.psum_tensor(f"e_bank{i}", [P, 512], F32)) for i in range(7)]
        h_ps, xt_ps, y_ps = bank[0:pairs], bank[pairs], bank[pairs + 1:]
        s = {n: sem(n) for n in (
            "w_in", "w_split", "w_ready", "zeros_ready", "pad_filled", "back_filled", "x_in", "xt_done", "x_hi_ready",
            "x_lo_ready", "h_done", "h_act_ready", "h_hi_ready", "h_lo_ready", "y_done", "y_out",
            "y_stored", "pool_passed", "pe_passed", "w8_in", "share_exp", "share_link", "ffn_ready")}
        block = ctx.enter_context(nc.Block())
        half_w = (W1 + W2) // 2

        def experts(eng, body):
            with eng.Fori(0, NE // 2) as pair:
                for par in range(2):
                    e = 2 * pair + par
                    items = eng.value_load(table[0:1, bass.ds(ITEMS + e, 1)], min_val=0, max_val=T // ROWS)
                    first = eng.value_load(table[0:1, bass.ds(FIRST + e, 1)], min_val=0, max_val=MAX_ITEMS)
                    body(e, par, items, first)

        @block.sync
        def _(sp):
            sp.dma_start(w8[:].bitcast(I32), io["ffn_w"]).then_inc(s["w8_in"], 16)
            sp.wait_ge(s["zeros_ready"], 1)
            for e in range(NE):
                row = sp.value_load(table[0:1, PAD_ROW + e:PAD_ROW + e + 1], min_val=e * REGION,
                                    max_val=e * REGION + T)
                sp.dma_start(dram["sent"][bass.ds(row, ROWS), :].rearrange("(r p) d -> p r d", p=P), zeros[:])\
                    .then_inc(s["pad_filled"], 16)
            sp.wait_ge(s["pad_filled"], 16 * NE)

            def body(e, par, items, first):
                with sp.Fori(0, items) as g:
                    i = first + g
                    sp.wait_ge(s["xt_done"], i + 1)
                    sp.dma_start(x_rows[:], dram["sent"][bass.ds(e * REGION + g * ROWS, ROWS), :]
                                 .rearrange("(r p) d -> p r d", p=P)).then_inc(s["x_in"], 16)

            experts(sp, body)
            total = sp.value_load(table[0:1, FIRST + NE:FIRST + NE + 1], min_val=0, max_val=MAX_ITEMS)
            sp.wait_ge(s["xt_done"], total + 1)
            sp.dma_start(x_rows[:], zeros_dram_view(dram)).then_inc(s["x_in"], 16)

        @block.gpsimd
        def _(pool):
            passed = Pass(pool, s["pool_passed"])
            nc.gpsimd.memset(zeros[:], 0.0).then_inc(s["zeros_ready"], 1)

            def split(e, par):
                pool.wait_ge(s["w_in"], 16 * (e + 1))
                passed()
                for n in range(2):
                    t = slice(n * half_w, (n + 1) * half_w)
                    nc.gpsimd.tensor_copy(w_hi[:, par, t], stage[:, t]).then_inc(s["w_split"], 1)
                    pool.wait_ge(s["w_split"], 2 * e + n + 1)
                    nc.gpsimd.tensor_tensor(w_lo[:, par, t], stage[:, t], w_hi[:, par, t].bitcast(F32),
                                            ALU.subtract).then_inc(s["w_ready"], 1)

            def load(e, source):
                pool.wait_ge(s["w_ready"], 2 * e)
                pool.dma_start(stage[:], io["w12"][source]).then_inc(s["w_in"], 16)

            pool.dma_start(stage[:], io["w12"][0]).then_inc(s["w_in"], 16)
            load(1, 1)
            split(1, 1)
            load(2, 2)
            passed.times = NE // 2 - 1
            with pool.Fori(1, NE // 2) as pair:
                for par in range(2):
                    e = 2 * pair + par
                    freed = pool.value_load(table[0:1, bass.ds(FIRST - 1 + e, 1)], min_val=0, max_val=MAX_ITEMS)
                    pool.wait_ge(s["y_done"], freed + 1)
                    split(e, par)
                    if par == 0:
                        load(e + 1, e + 1)
                    else:
                        load(e + 1, pool.snap((e + 1) % NE))
            pool.wait_ge(s["w_in"], 16 * (NE + 1))
            passed.done()

        @block.scalar
        def _(act):
            act.sem_inc(s["h_act_ready"], 1)
            act.sem_inc(s["y_out"], 1)
            act.sem_inc(s["y_stored"], 16)
            nc.scalar.activation(share[:, 1], gap_all[:], ACT.Exp).then_inc(s["share_exp"], 1)

            def x_parts(i):
                act.wait_ge(s["xt_done"], i + 2)
                for k in range(KD):
                    nc.scalar.activation(x_hi[:, k], xt_ps[:, k * ROWS:(k + 1) * ROWS], ACT.Copy,
                                         scale=moe_w[:, k:k + 1]).then_inc(s["x_hi_ready"], 1)

            act.wait_ge(s["w_in"], 16)
            for n in range(2):
                t = slice(n * half_w, (n + 1) * half_w)
                nc.scalar.activation(w_hi[:, 0, t], stage[:, t], ACT.Copy).then_inc(s["w_split"], 1)
            x_parts(0)
            act.wait_ge(s["zeros_ready"], 1)
            for n in range(T * 2 // ROWS, MAX_ITEMS):
                act.dma_start(dram["back"][n * ROWS:(n + 1) * ROWS, :].rearrange("(r p) d -> p r d", p=P), zeros[:])\
                    .then_inc(s["back_filled"], 16)

            def body(e, par, items, first):
                with act.Fori(0, items) as g:
                    i = first + g
                    for p in range(pairs):
                        act.wait_ge(s["h_done"], pairs * i + p + 1)
                        act.wait_ge(s["h_lo_ready"], pairs * i + p if p else pairs * i + 1)
                        nc.scalar.activation(h_act[:, p % 2], h_ps[p][:], ACT.Silu)\
                            .then_inc(s["h_act_ready"], 1)
                    x_parts(i + 1)
                    act.wait_ge(s["y_stored"], 16 * (i + 1))
                    act.wait_ge(s["y_done"], i + 2)
                    for r in range(RT):
                        nc.scalar.activation(y_rows[:, r, :], y_ps[r][:, 0:D], ACT.Copy).then_inc(s["y_out"], 1)
                    act.wait_ge(s["y_out"], RT * (i + 1) + 1)
                    act.wait_ge(s["back_filled"], 16 * (MAX_ITEMS - T * 2 // ROWS))
                    at = nc.s_assert_within(i, 0, MAX_ITEMS - 1, skip_runtime_bounds_check_because=
                                            "two rows a token and each expert's last item padded: 39 items at most")
                    act.dma_start(dram["back"][bass.ds(at * ROWS, ROWS), :]
                                  .rearrange("(r p) d -> p r d", p=P), y_rows[:]).then_inc(s["y_stored"], 16)

            experts(act, body)
            total = act.value_load(table[0:1, FIRST + NE:FIRST + NE + 1], min_val=0, max_val=MAX_ITEMS)
            act.wait_ge(s["y_stored"], 16 * (total + 1))
            nc.scalar.activation(y_rows[:, 0, 0:1], y_rows[:, 0, 1:2], ACT.Copy)

        @block.tensor
        def _(pe):
            passed = Pass(pe, s["pe_passed"])
            passed.times = NE // 2
            pe.sem_inc(s["xt_done"], 1)
            pe.sem_inc(s["y_done"], 1)
            mm = nc.tensor.matmul

            def transposes(i):
                pe.wait_ge(s["x_in"], 16 * (i + 1))
                for k in range(KD):
                    for r in range(RT):
                        t = nc.tensor.transpose(xt_ps[:, k * ROWS + r * P:k * ROWS + (r + 1) * P],
                                                x_rows[:, r, k * P:(k + 1) * P], ident[:])
                t.then_inc(s["xt_done"], 1)

            transposes(0)

            def body(e, par, items, first):
                pe.wait_ge(s["w_ready"], 2 * (e + 1))
                passed()
                w1h = w_hi[:, par, 0:W1].rearrange("p (k f) -> p k f", k=KD)
                w1l = w_lo[:, par, 0:W1].rearrange("p (k f) -> p k f", k=KD)
                w2h = w_hi[:, par, W1:].rearrange("p (k d) -> p k d", k=KF)
                w2l = w_lo[:, par, W1:].rearrange("p (k d) -> p k d", k=KF)
                with pe.Fori(0, items) as g:
                    i = first + g
                    pe.wait_ge(s["x_lo_ready"], KD * (i + 1))
                    for p in range(pairs):
                        pe.wait_ge(s["h_act_ready"], pairs * i + 1)
                        for n in range(2):
                            f = 2 * p + n
                            out = h_ps[p][:, n * ROWS:(n + 1) * ROWS]
                            for k in range(KD):
                                t = slice(f * P, (f + 1) * P)
                                mm(out, w1h[:, k, t], x_hi[:, k], start=k == 0, stop=False)
                                mm(out, w1h[:, k, t], x_lo[:, k], start=False, stop=False)
                                r = mm(out, w1l[:, k, t], x_hi[:, k], start=False, stop=k == KD - 1)
                        r.then_inc(s["h_done"], 1)
                    transposes(i + 1)
                    pe.wait_ge(s["y_out"], RT * i + 1)
                    order = [(r, p) for r in range(RT) for p in range(pairs - 1)] + [(r, pairs - 1) for r in range(RT)]
                    for r, p in order:
                        pe.wait_ge(s["h_lo_ready"], pairs * i + p + 2)
                        for k in (2 * p, 2 * p + 1):
                            t = slice(r * P, (r + 1) * P)
                            out = y_ps[r][:, 0:D]
                            mm(out, h_hi[:, k, t], w2h[:, k], start=k == 0, stop=False)
                            mm(out, h_hi[:, k, t], w2l[:, k], start=False, stop=False)
                            m = mm(out, h_lo[:, k, t], w2h[:, k], start=False, stop=k == KF - 1)
                    m.then_inc(s["y_done"], 1)

            experts(pe, body)
            passed.done()

        @block.vector
        def _(dve):
            tt, stt, ts = nc.vector.tensor_tensor, nc.vector.scalar_tensor_tensor, nc.vector.tensor_scalar
            dve.sem_inc(s["h_lo_ready"], 1)
            dve.wait_ge(s["share_exp"], 1)
            link = Link(dve, s["share_link"], 0)
            link(ts(share[:, 0], share[:, 1], 1.0, None, ALU.add))
            link(nc.vector.reciprocal(share[:, 0], share[:, 0]))
            link(tt(share[:, 1], share[:, 1], share[:, 0], ALU.mult))
            rows = routing["rows"]
            for e in range(1, NE):
                link(ts(moved[:], rows[:], float(e * REGION), routing["step"][:, e - 1:e], ALU.is_ge, ALU.mult))
                link(tt(shift[:], shift[:], moved[:], ALU.add) if e > 1 else nc.vector.tensor_copy(shift[:], moved[:]))
            tt(routing["back_rows"][:], rows[:], shift[:], ALU.add).then_inc(s["ffn_ready"], 1)
            for n in range(2):
                t = slice(n * half_w, (n + 1) * half_w)
                dve.wait_ge(s["w_split"], n + 1)
                tt(w_lo[:, 0, t], stage[:, t], w_hi[:, 0, t].bitcast(F32), ALU.subtract).then_inc(s["w_ready"], 1)

            def x_parts(i):
                dve.wait_ge(s["x_hi_ready"], KD * (i + 1))
                for k in range(KD):
                    stt(x_lo[:, k], xt_ps[:, k * ROWS:(k + 1) * ROWS], moe_w[:, k:k + 1], x_hi[:, k].bitcast(F32),
                        ALU.mult, ALU.subtract).then_inc(s["x_lo_ready"], 1)

            x_parts(0)
            dve.wait_ge(s["w8_in"], 16)
            nc.vector.tensor_copy(cst["ffn_w"][:], w8[:]).then_inc(s["ffn_ready"], 1)

            def body(e, par, items, first):
                with dve.Fori(0, items) as g:
                    i = first + g
                    dve.wait_ge(s["y_done"], i + 1)
                    for p in range(pairs):
                        n = pairs * i + p
                        dve.wait_ge(s["h_act_ready"], n + 2)
                        nc.vector.tensor_copy(flat(h_hi[:, 2 * p:2 * p + 2]), h_act[:, p % 2])\
                            .then_inc(s["h_hi_ready"], 1)
                        dve.wait_ge(s["h_hi_ready"], n + 1)
                        tt(flat(h_lo[:, 2 * p:2 * p + 2]), h_act[:, p % 2],
                           flat(h_hi[:, 2 * p:2 * p + 2]).bitcast(F32), ALU.subtract).then_inc(s["h_lo_ready"], 1)
                    x_parts(i + 1)

            experts(dve, body)


def zeros_dram_view(dram):
    return dram["sent"][0:ROWS, :].rearrange("(r p) d -> p r d", p=P)


def ffn_phase(nc, io, dram, cst, routing, out):
    with ExitStack() as ctx:
        def sb(name, shape, dt=F32):
            return ctx.enter_context(nc.sbuf_tensor("f_" + name, shape, dt))

        def sem(name):
            return ctx.enter_context(nc.semaphore("f_" + name))

        ident, half, w = cst["ident"], cst["half"], cst["ffn_w"]
        wg = w[:, 0:KD * FF].rearrange("p (k f) -> p k f", k=KD)
        wu = w[:, KD * FF:2 * KD * FF].rearrange("p (k f) -> p k f", k=KD)
        wd = w[:, 2 * KD * FF:].rearrange("p (k d) -> p k d", k=KF)
        s_gu = sb("s_gu", [P, 2, KF])
        s_down = sb("s_down", [P, D])
        row_u = sb("f_row_u", [P, 2, 2 * CH], U32)
        back = sb("back", [P, 2, CH, 2, D])
        res = sb("res", [P, 2, CH, D])
        mixed = sb("mixed", [P, CH, D])
        bn = sb("bn", [P, 2, CH, 6])
        mv = sb("mv", [P, CH, 2])
        norm = sb("norm", [P, 3, CH])
        x1 = sb("x1", [P, 2, CH, D])
        x_hi = sb("f_x_hi", [P, KD, GT], F32R)
        x_lo = sb("f_x_lo", [P, KD, GT], F32R)
        gate = sb("gate", [P, 2, GT])
        fused = sb("fused", [P, FUSED, GT])
        f_hi = sb("f_hi", [P, KF, GT], F32R)
        f_lo = sb("f_lo", [P, KF, GT], F32R)
        y = sb("y", [P, CH, D])
        mv2 = sb("mv2", [P, CH, 2])
        norm2 = sb("norm2", [P, 3, CH])
        out_t = sb("out_t", [P, CH, D])
        rows_all, share = routing["back_rows"], routing["share"]
        bank = [ctx.enter_context(nc.psum_tensor(f"f_bank{i}", [P, 512], F32)) for i in range(8)]
        gate_ps, up_ps, xt_ps, down_ps = bank[0:2], bank[2:4], bank[4:6], bank[6:8]
        s = {n: sem(n) for n in (
            "scales_in", "rows_ready", "back_in0", "back_in1", "res_in0", "res_in1", "mixed_one", "mixed_both",
            "mix_stats", "mix_moments", "var_ready", "rs_ready", "shift_ready", "x1_ready",
            "xt_done", "x_hi_ready", "x_lo_ready", "gate_done", "up_done", "gate_ready", "fused_ready",
            "f_hi_ready", "pool_lo", "dve_lo", "down_done", "y_scaled", "y_ready", "y_stats", "y_moments",
            "var2_ready", "rs2_ready", "shift2_ready", "out_ready", "out_free", "out_stored", "pool_passed",
            "dve_passed")}
        block = ctx.enter_context(nc.Block())

        def groups(eng, group):
            group(0, 0, 0)
            with eng.Fori(0, PAIRS) as b:
                group(2 * b + 1, 1, b)
                group(2 * b + 2, 0, b + 1)
            for g in range(2 * PAIRS + 1, NG):
                group(g, g % 2, g // 2)

        def last(g, ahead):
            return isinstance(g, int) and g + ahead >= NG

        def first(g):
            return isinstance(g, int) and g == 0

        @block.sync
        def _(sp):
            sp.dma_start(s_gu[:], io["s_gu"]).then_inc(s["scales_in"], 16)
            sp.dma_start(s_down[:], io["s_down"].partition_broadcast(P)).then_inc(s["scales_in"], 16)
            sp.sem_inc(s["out_free"], 1)

            def fetch(g, j):
                if not (isinstance(g, int) and g < 2):
                    sp.wait_ge(s["var_ready"], g - 1)
                sp.dma_start(res[:, j], dram["x_res"][g]).then_inc(s[f"res_in{j}"], 16)

            def store(g):
                sp.wait_ge(s["out_ready"], g + 2)
                sp.dma_start(out[g], out_t[:]).then_inc(s["out_stored"], 16)
                sp.wait_ge(s["out_stored"], 16 * (g + 1))
                sp.sem_inc(s["out_free"], 1)

            def group(g, j, h):
                if not last(g, 2):
                    fetch(g + 2, j)
                if not first(g):
                    store(g - 1)

            fetch(0, 0)
            fetch(1, 1)
            groups(sp, group)
            store(NG - 1)

        @block.gpsimd
        def _(pool):
            passed = Pass(pool, s["pool_passed"])

            def gather(g, j, n):
                if n == 0:
                    pool.wait_ge(s["rows_ready"], g + 1)
                    if not (isinstance(g, int) and g < 2):
                        pool.wait_ge(s["var_ready"], g - 1)
                        passed()
                nc.gpsimd.indirect_dma_start(
                    out=back[:, j, n // 2, n % 2, :], out_offset=None, in_=dram["back"],
                    in_offset=bass.IndirectOffsetOnAxis(ap=row_u[:, j, n:n + 1], axis=0))\
                    .then_inc(s[f"back_in{j}"], 16)

            def deviation(g, tile, ready, done):
                pool.wait_ge(s[ready], g + 1)
                nc.gpsimd.tensor_tensor(tile[:, 1], tile[:, 0], half[:], ALU.pow).then_inc(s[done], 1)

            def part(g, f):
                pool.wait_ge(s["f_hi_ready"], KF * g + f + 1)
                nc.gpsimd.tensor_tensor(f_lo[:, f], fused[:, f % FUSED], f_hi[:, f].bitcast(F32), ALU.subtract)\
                    .then_inc(s["pool_lo"], 1)

            def group(g, j, h):
                for f in range(KF):
                    if f == MIX_NORM + (MIX_LATE if first(g) else 0) and not last(g, 1):
                        deviation(g + 1, norm, "var_ready", "rs_ready")
                    if f == Y_NORM and not first(g):
                        deviation(g - 1, norm2, "var2_ready", "rs2_ready")
                    if not last(g, 2):
                        gather(g + 2, j, f)
                    if 1 <= f <= POOL_PARTS:
                        part(g, f - 1)

            for n in range(2 * CH):
                gather(0, 0, n)
            deviation(0, norm, "var_ready", "rs_ready")
            for n in range(2 * CH):
                gather(1, 1, n)

            def counted(g, j, h):
                passed.times = 1 if isinstance(g, int) else PAIRS
                group(g, j, h)

            groups(pool, counted)
            passed.times = 1
            deviation(NG - 1, norm2, "var2_ready", "rs2_ready")
            passed.done()

        @block.scalar
        def _(act):
            act.wait_ge(s["scales_in"], 32)
            act.sem_inc(s["out_ready"], 1)

            def normalize(to, x, tile, done):
                for c in range(CH):
                    i = nc.scalar.activation(to[:, c], x[:, c], ACT.Identity, bias=tile[:, 2, c:c + 1],
                                             scale=tile[:, 1, c:c + 1])
                i.then_inc(s[done], 1)

            def scale1(g, j):
                act.wait_ge(s["shift_ready"], g + 1)
                if not (isinstance(g, int) and g < 2):
                    act.wait_ge(s["y_ready"], g - 1)
                normalize(x1[:, j], mixed, norm, "x1_ready")

            def scale2(g):
                act.wait_ge(s["shift2_ready"], g + 1)
                act.wait_ge(s["out_free"], g + 1)
                normalize(out_t, y, norm2, "out_ready")

            def x_parts(g):
                for k in range(KD):
                    act.wait_ge(s["xt_done"], KD * g + k + 1)
                    nc.scalar.activation(x_hi[:, k], xt_ps[k][:], ACT.Copy).then_inc(s["x_hi_ready"], 1)

            def part(g, f):
                act.wait_ge(s["fused_ready"], KF * g + f + 1)
                nc.scalar.activation(f_hi[:, f], fused[:, f % FUSED], ACT.Copy).then_inc(s["f_hi_ready"], 1)

            def group(g, j, h):
                for f in range(KF):
                    n = KF * g + f
                    act.wait_ge(s["gate_done"], n + 1)
                    wait(act, s["fused_ready"], n - 1 if f else KF * g)
                    nc.scalar.activation(gate[:, f % 2], gate_ps[f % 2][:], ACT.Silu, scale=s_gu[:, 0, f:f + 1])\
                        .then_inc(s["gate_ready"], 1)
                    if f:
                        part(g, f - 1)
                    if f == MIX_NORM + 1 + (1 if first(g) else 0) and not last(g, 1) and not first(g):
                        scale1(g + 1, 1 - j)
                part(g, KF - 1)
                if first(g):
                    scale1(1, 1)
                if not last(g, 1):
                    x_parts(g + 1)
                if not first(g):
                    scale2(g - 1)

            scale1(0, 0)
            x_parts(0)
            groups(act, group)
            scale2(NG - 1)

        @block.tensor
        def _(pe):
            mm = nc.tensor.matmul

            def transposes(g, j):
                pe.wait_ge(s["x1_ready"], g + 1)
                wait(pe, s["x_lo_ready"], KD * g)
                for k in range(KD):
                    for c in range(CH):
                        i = nc.tensor.transpose(xt_ps[k][:, c * P:(c + 1) * P], x1[:, j, c, k * P:(k + 1) * P],
                                                ident[:])
                    i.then_inc(s["xt_done"], 1)

            def units(g):
                pe.wait_ge(s["x_lo_ready"], KD * (g + 1))
                for f in range(KF):
                    n = KF * g + f
                    t = slice(f * P, (f + 1) * P)
                    for w_t, ps, done, freed in ((wg, gate_ps, "gate_done", "gate_ready"),
                                                 (wu, up_ps, "up_done", "fused_ready")):
                        wait(pe, s[freed], n - 1 if f else KF * g)
                        for k in range(KD):
                            mm(ps[f % 2][:], w_t[:, k, t], x_hi[:, k], start=k == 0, stop=False)
                            i = mm(ps[f % 2][:], w_t[:, k, t], x_lo[:, k], start=False, stop=k == KD - 1)
                        i.then_inc(s[done], 1)

            def down(g):
                wait(pe, s["y_scaled"], g)
                for c in range(CH):
                    o = down_ps[c // 2][:, (c % 2) * D:(c % 2 + 1) * D]
                    for k in range(KF):
                        if c == 0 and k < POOL_PARTS:
                            pe.wait_ge(s["pool_lo"], POOL_PARTS * g + k + 1)
                        elif c == 0:
                            pe.wait_ge(s["dve_lo"], (KF - POOL_PARTS) * g + k - POOL_PARTS + 1)
                        t = slice(c * P, (c + 1) * P)
                        mm(o, f_hi[:, k, t], wd[:, k], start=k == 0, stop=False)
                        i = mm(o, f_lo[:, k, t], wd[:, k], start=False, stop=k == KF - 1)
                    i.then_inc(s["down_done"], 1)

            def group(g, j, h):
                units(g)
                if not last(g, 1):
                    transposes(g + 1, 1 - j)
                down(g)

            transposes(0, 0)
            groups(pe, group)

        @block.vector
        def _(dve):
            passed = Pass(dve, s["dve_passed"])
            tt, stt, ts = nc.vector.tensor_tensor, nc.vector.scalar_tensor_tensor, nc.vector.tensor_scalar
            dve.wait_ge(s["scales_in"], 32)

            def rows(g, j):
                nc.vector.tensor_copy(row_u[:, j], rows_all[:, bass.ds(2 * CH * g, 2 * CH)])\
                    .then_inc(s["rows_ready"], 1)

            def mix_first(g, j, h):
                dve.wait_ge(s[f"back_in{j}"], 16 * 2 * CH * (h + 1))
                dve.wait_ge(s[f"res_in{j}"], 16 * (h + 1))
                wait(dve, s["x1_ready"], g)
                passed()
                for c in range(CH):
                    i = stt(mixed[:, c], back[:, j, c, 0], share[:, 0, bass.ds(CH * g + c, 1)], res[:, j, c],
                            ALU.mult, ALU.add)
                i.then_inc(s["mixed_one"], 1)

            def mix_second(g, j, h):
                dve.wait_ge(s["mixed_one"], g + 1)
                passed()
                for c in range(CH):
                    i = stt(mixed[:, c], back[:, j, c, 1], share[:, 1, bass.ds(CH * g + c, 1)], mixed[:, c],
                            ALU.mult, ALU.add)
                i.then_inc(s["mixed_both"], 1)

            def stats(g, n, x, ready, done):
                dve.wait_ge(s[ready], g + 1)
                passed()
                for c in range(CH):
                    i = nc.vector.bn_stats(bn[:, n, c], x[:, c])
                i.then_inc(s[done], 1)

            def moments(g, n, to, ready, done):
                dve.wait_ge(s[ready], g + 1)
                passed()
                for c in range(CH):
                    i = nc.vector.bn_aggr(to[:, c], bn[:, n, c])
                i.then_inc(s[done], 1)

            def variance(g, to, tile, ready, done):
                dve.wait_ge(s[ready], g + 1)
                ts(tile[:, 0], to[:, :, 1], LN_EPS, None, ALU.add).then_inc(s[done], 1)

            def shift(g, to, tile, ready, done):
                dve.wait_ge(s[ready], g + 1)
                stt(tile[:, 2], to[:, :, 0], -1.0, tile[:, 1], ALU.mult, ALU.mult).then_inc(s[done], 1)

            def scale_down(g, j):
                dve.wait_ge(s["down_done"], CH * (g + 1))
                dve.wait_ge(s["out_ready"], g + 1)
                for n in range(CH // 2):
                    i = tt(y[:, 2 * n:2 * n + 2], down_ps[n][:].rearrange("p (c d) -> p c d", c=2),
                           bcast(s_down[:], 1, 2), ALU.mult)
                i.then_inc(s["y_scaled"], 1)

            def add_x1(g, j):
                dve.wait_ge(s["y_scaled"], g + 1)
                tt(y[:], y[:], x1[:, j], ALU.add).then_inc(s["y_ready"], 1)

            def x_parts(g):
                for k in range(KD):
                    dve.wait_ge(s["x_hi_ready"], KD * g + k + 1)
                    tt(x_lo[:, k], xt_ps[k][:], x_hi[:, k].bitcast(F32), ALU.subtract)\
                        .then_inc(s["x_lo_ready"], 1)

            def fuse(g, f):
                n = KF * g + f
                dve.wait_ge(s["up_done"], n + 1)
                dve.wait_ge(s["gate_ready"], n + 1)
                if f >= FUSED:
                    dve.wait_ge(s["pool_lo"], POOL_PARTS * g + f - FUSED + 1)
                elif f == 0:
                    wait(dve, s["pool_lo"], POOL_PARTS * g)
                elif f == 1:
                    wait(dve, s["dve_lo"], (KF - POOL_PARTS) * g)
                stt(fused[:, f % FUSED], up_ps[f % 2][:], s_gu[:, 1, f:f + 1], gate[:, f % 2], ALU.mult, ALU.mult)\
                    .then_inc(s["fused_ready"], 1)

            def part(g, f):
                dve.wait_ge(s["f_hi_ready"], KF * g + f + 1)
                tt(f_lo[:, f], fused[:, f % FUSED], f_hi[:, f].bitcast(F32), ALU.subtract)\
                    .then_inc(s["dve_lo"], 1)

            def mix_step(n, g, j, h):
                if n == 0:
                    mix_first(g, j, h)
                if n == 1:
                    mix_second(g, j, h)
                if n == 2:
                    stats(g, 0, mixed, "mixed_both", "mix_stats")
                if n == 3:
                    moments(g, 0, mv, "mix_stats", "mix_moments")
                    variance(g, mv, norm, "mix_moments", "var_ready")
                if n == 4:
                    shift(g, mv, norm, "rs_ready", "shift_ready")

            def y_step(n, g, j):
                if n == 2:
                    scale_down(g, j)
                if n == 3:
                    add_x1(g, j)
                if n == 5:
                    stats(g, 1, y, "y_ready", "y_stats")
                if n == 6:
                    moments(g, 1, mv2, "y_stats", "y_moments")
                    variance(g, mv2, norm2, "y_moments", "var2_ready")
                if n == 7:
                    shift(g, mv2, norm2, "rs2_ready", "shift2_ready")

            def group(g, j, h):
                passed.times = 1 if isinstance(g, int) else PAIRS
                for f in range(KF):
                    fuse(g, f)
                    if f == 0 and not last(g, 2):
                        rows(g + 2, j)
                    if not first(g):
                        y_step(f, g - 1, 1 - j)
                    if not last(g, 1):
                        mix_step(f - (MIX_LATE if first(g) else 0), g + 1, 1 - j, h + j)
                    if f > POOL_PARTS:
                        part(g, f - 1)
                part(g, KF - 1)
                if not last(g, 1):
                    x_parts(g + 1)

            rows(0, 0)
            rows(1, 1)
            for n in range(5):
                mix_step(n, 0, 0, 0)
            x_parts(0)
            groups(dve, group)
            passed.times = 1
            for n in range(KF):
                y_step(n, NG - 1, (NG - 1) % 2)
            passed.done()


def build(nc, io, out):
    dram = {
        "sent": nc.dram_tensor("sent_rows", [NE * REGION, D], F32, kind="Internal").ap(),
        "back": nc.dram_tensor("back_rows", [MAX_ITEMS * ROWS, D], F32, kind="Internal").ap(),
        "x_res": nc.dram_tensor("x_res_dram", [NG, P, CH, D], F32, kind="Internal").ap(),
    }
    with ExitStack() as ctx:
        def sb(name, shape, dt=F32):
            return ctx.enter_context(nc.sbuf_tensor(name, shape, dt))

        cst = {n: sb(n, [P, P]) for n in ("ident", "le", "gt", "lt", "ones")}
        cst["half"] = sb("half", [P, CH])
        cst["zero1"] = sb("zero1", [P, 1])
        cst["moe_w"] = sb("moe_w", [P, KD])
        routing = {
            "rows": sb("rows_all", [P, 2 * CH * NG]),
            "back_rows": sb("back_rows_all", [P, 2 * CH * NG], U32),
            "step": sb("region_step", [P, NE]),
            "gap": sb("gap_all", [P, CH * NG]),
            "share": sb("share", [P, 2, CH * NG]),
            "table": sb("table", [1, TABLE], I32),
        }
        cst["started"] = ctx.enter_context(nc.semaphore("constants_ready"))
        with nc.semaphore("filled") as filled, nc.Block() as block:
            @block.gpsimd
            def _(pool):
                nc.gpsimd.memset(cst["zero1"][:], 0.0)
                nc.gpsimd.memset(cst["half"][:], -0.5)
                for n in ("ident", "le", "gt", "lt", "ones"):
                    i = nc.gpsimd.memset(cst[n][:], 0.0 if n == "ident" else 1.0)
                i.then_inc(filled, 1)
                pool.wait_ge(filled, 1)
                for n, op, mult, step in (("ident", ALU.not_equal, 1, -1), ("le", ALU.is_ge, -1, 1),
                                          ("gt", ALU.is_gt, 1, -1), ("lt", ALU.is_gt, -1, 1)):
                    m = cst[n][:]
                    i = nc.gpsimd.affine_select(out=m, in_=m, compare_op=op, fill=1.0 if n == "ident" else 0.0,
                                                base=0, pattern=[[step, P]], channel_multiplier=mult)
                i.then_inc(cst["started"], 1)
                pool.wait_ge(cst["started"], 1)
        mamba_phase(nc, io, dram, cst, routing)
        cst["ffn_w"] = sb("ffn_w", [P, FFN_W], F32R)
        expert_phase(nc, io, dram, cst, routing)
        ffn_phase(nc, io, dram, cst, routing, out)


def kernel(**inputs):
    import numpy as np
    import concourse.bacc as bacc
    from concourse.bass_utils import run_bass_kernel_spmd

    def arr(name):
        return np.asarray(inputs[name])

    def cols(a, k):
        return np.ascontiguousarray(np.moveaxis(a.reshape(k, P, *a.shape[1:]), 0, 1))

    w1 = arr("L0_attn_w1").transpose(0, 2, 1).reshape(NE, KD, P, FF).transpose(0, 2, 1, 3).reshape(NE, P, KD * FF)
    w2 = arr("L0_attn_w2").transpose(0, 2, 1).reshape(NE, KF, P, D).transpose(0, 2, 1, 3).reshape(NE, P, KF * D)
    ffn = [cols(arr("L0_ffn_w_gate"), KD), cols(arr("L0_ffn_w_up"), KD), cols(arr("L0_ffn_w_down"), KF)]
    arrays = {
        "x": arr("L0_attn_x").reshape(NG, CH, P, D).transpose(0, 2, 1, 3),
        "in_w": cols(arr("L0_attn_in_proj_w").T, KD),
        "out_w": cols(arr("L0_attn_out_proj_w").T, KI),
        "gate_w": cols(arr("L0_attn_gate_w").T, KD),
        "conv_w": cols(arr("L0_attn_conv_w"), KC),
        "conv_b": cols(arr("L0_attn_conv_b"), KC),
        "d_col": cols(np.repeat(arr("L0_attn_D"), HD), KI),
        "ssm_w": cols(arr("L0_attn_ssm_norm_w"), KI),
        "nm_w": cols(arr("L0_attn_norm_mamba_w"), KD),
        "moe_w": cols(arr("L0_attn_norm_moe_w"), KD),
        "dt_bias": arr("L0_attn_dt_bias"),
        "a_log": arr("L0_attn_A_log"),
        "w12": np.concatenate([w1, w2], axis=2),
        "ffn_w": np.ascontiguousarray(np.concatenate([a.reshape(P, -1) for a in ffn], axis=1)).view(np.int32),
        "s_gu": np.stack([cols(arr("L0_ffn_s_gate"), KF), cols(arr("L0_ffn_s_up"), KF)], axis=1),
        "s_down": arr("L0_ffn_s_down"),
    }
    arrays = {f"in_{n}": np.ascontiguousarray(a) for n, a in arrays.items()}
    nc = bacc.Bacc("TRN2", target_bir_lowering=False, num_devices=1)
    io = {n[3:]: nc.dram_tensor(n, a.shape, mybir.dt.from_np(a.dtype), kind="ExternalInput").ap()
          for n, a in arrays.items()}
    out = nc.dram_tensor("out", [NG, P, CH, D], F32, kind="ExternalOutput").ap()
    build(nc, io, out)
    r = run_bass_kernel_spmd(nc, [arrays], core_ids=[0])
    got = r.results[0]["out"]
    return np.ascontiguousarray(np.asarray(got).transpose(0, 2, 1, 3)).reshape(B, L, D)
```
